# Optimizing a Trainium2 kernel written in Bass

```python
import numpy as np
import jax
import jax.numpy as jnp

def _softmax(x, axis=-1):
    return jax.nn.softmax(x, axis=axis)

def _gelu(x):
    return jax.nn.gelu(x, approximate=True)

def _silu(x):
    return jax.nn.silu(x)

def _sigmoid(x):
    return jax.nn.sigmoid(x)

def _layernorm(x, axis=-1, eps=1e-05):
    m = jnp.mean(x, axis=axis, keepdims=True)
    v = jnp.var(x, axis=axis, keepdims=True)
    return (x - m) / jnp.sqrt(v + eps)

def _scatter_add(tgt, idx, src, axis=0):
    return tgt.at[idx].add(src)

def _segment_sum(src, seg, n):
    return jax.ops.segment_sum(src, seg, n)
kernel_name = 'mk_adaln_d1_jaxref_r8_4522d5'

def setup_inputs(seed: int=0):
    np.random.seed(seed)
    _w = jnp.asarray

    def _L0_attn_setup():
        import jax, jax.numpy as jnp
        import numpy as np
        import math
        H = 16
        N_EMBD = 128
        EPS = 1e-05
        key = jax.random.key(seed)
        ks = jax.random.split(key, 6)
        B, T, C = (2, 256, 128)
        x = jax.random.normal(ks[0], (B, T, C), dtype=jnp.float32)
        s = 0.02
        Wq = jax.random.normal(ks[1], (C, N_EMBD), dtype=jnp.float32) * s
        Wk = jax.random.normal(ks[2], (C, N_EMBD), dtype=jnp.float32) * s
        Wv = jax.random.normal(ks[3], (C, N_EMBD), dtype=jnp.float32) * s
        Wo = jax.random.normal(ks[4], (N_EMBD, C), dtype=jnp.float32) * s
        return {'x': x, 'Wq': Wq, 'bq': jnp.zeros((N_EMBD,), jnp.float32), 'Wk': Wk, 'bk': jnp.zeros((N_EMBD,), jnp.float32), 'Wv': Wv, 'bv': jnp.zeros((N_EMBD,), jnp.float32), 'Wo': Wo, 'bo': jnp.zeros((C,), jnp.float32), 'gamma': jnp.ones((C,), jnp.float32), 'beta': jnp.zeros((C,), jnp.float32)}
    _L0_attn_in = _L0_attn_setup()

    def _L0_ffn_setup():
        import jax, jax.numpy as jnp
        import numpy as np
        TOP_K = 2
        TEMP = 0.9
        EPS = 1e-05
        B, S, D, F, E = (2, 256, 128, 512, 8)

        def _moe_forward(x, gate_w, gate_b, w1, b1, w2, b2, ln_g, ln_b):
            logits = (x @ gate_w + gate_b) / TEMP
            topk_vals, topk_idx = jax.lax.top_k(logits, TOP_K)
            keep = jax.nn.one_hot(topk_idx, E, dtype=jnp.bool_).any(-2)
            masked = jnp.where(keep, logits, -jnp.inf)
            gate_probs = jax.nn.softmax(masked, axis=-1)
            h = jnp.einsum('bsd,edf->bsef', x, w1) + b1
            h = jax.nn.gelu(h, approximate=False)
            expert_out = jnp.einsum('bsef,efd->bsed', h, w2) + b2
            out = jnp.einsum('bse,bsed->bsd', gate_probs, expert_out)
            mu = out.mean(-1, keepdims=True)
            var = out.var(-1, keepdims=True)
            out = (out - mu) / jnp.sqrt(var + EPS) * ln_g + ln_b
            return out
        key = jax.random.key(seed)
        ks = jax.random.split(key, 4)
        scale_in = 1.0 / np.sqrt(D)
        scale_ff = 1.0 / np.sqrt(F)
        return {'x': jax.random.normal(ks[0], (B, S, D), jnp.float32), 'gate_w': jax.random.normal(ks[1], (D, E), jnp.float32) * scale_in, 'gate_b': jnp.zeros((E,), jnp.float32), 'w1': jax.random.normal(ks[2], (E, D, F), jnp.float32) * scale_in, 'b1': jnp.zeros((E, F), jnp.float32), 'w2': jax.random.normal(ks[3], (E, F, D), jnp.float32) * scale_ff, 'b2': jnp.zeros((E, D), jnp.float32), 'ln_g': jnp.ones((D,), jnp.float32), 'ln_b': jnp.zeros((D,), jnp.float32)}
    _L0_ffn_in = _L0_ffn_setup()
    _L0_c = _w((lambda *s: np.random.randn(*s).astype(np.float32) * 0.05)(4, 128))
    _L0_wmod = _w((lambda *s: np.random.randn(*s).astype(np.float32) * 0.05)(128, 6 * 128) * 128 ** (-0.5))
    _d = {'L0_attn_x': _L0_attn_in['x'], 'L0_attn_Wq': _L0_attn_in['Wq'], 'L0_attn_bq': _L0_attn_in['bq'], 'L0_attn_Wk': _L0_attn_in['Wk'], 'L0_attn_bk': _L0_attn_in['bk'], 'L0_attn_Wv': _L0_attn_in['Wv'], 'L0_attn_bv': _L0_attn_in['bv'], 'L0_attn_Wo': _L0_attn_in['Wo'], 'L0_attn_bo': _L0_attn_in['bo'], 'L0_attn_gamma': _L0_attn_in['gamma'], 'L0_attn_beta': _L0_attn_in['beta'], 'L0_ffn_gate_w': _L0_ffn_in['gate_w'], 'L0_ffn_gate_b': _L0_ffn_in['gate_b'], 'L0_ffn_w1': _L0_ffn_in['w1'], 'L0_ffn_b1': _L0_ffn_in['b1'], 'L0_ffn_w2': _L0_ffn_in['w2'], 'L0_ffn_b2': _L0_ffn_in['b2'], 'L0_ffn_ln_g': _L0_ffn_in['ln_g'], 'L0_ffn_ln_b': _L0_ffn_in['ln_b'], 'L0_c': _L0_c, 'L0_wmod': _L0_wmod}
    _x0 = _d['L0_attn_x']
    _d['L0_attn_x'] = jax.random.normal(jax.random.fold_in(jax.random.key(seed), 1), (4, 512, 128), dtype=_x0.dtype)
    del _x0
    return _d

def reference(L0_attn_x, L0_attn_Wq, L0_attn_bq, L0_attn_Wk, L0_attn_bk, L0_attn_Wv, L0_attn_bv, L0_attn_Wo, L0_attn_bo, L0_attn_gamma, L0_attn_beta, L0_ffn_gate_w, L0_ffn_gate_b, L0_ffn_w1, L0_ffn_b1, L0_ffn_w2, L0_ffn_b2, L0_ffn_ln_g, L0_ffn_ln_b, L0_c, L0_wmod):

    def _L0_attn_ref(x, Wq, bq, Wk, bk, Wv, bv, Wo, bo, gamma, beta):
        import jax, jax.numpy as jnp
        import numpy as np
        import math
        H = 16
        N_EMBD = 128
        EPS = 1e-05
        B, T, _ = x.shape
        Dh = N_EMBD // H

        def split_heads(y):
            return y.reshape(B, T, H, Dh).transpose(0, 2, 1, 3)
        q = split_heads(x @ Wq + bq)
        k = split_heads(x @ Wk + bk)
        v = split_heads(x @ Wv + bv)
        att = jnp.einsum('bhtd,bhsd->bhts', q, k) * (1.0 / math.sqrt(Dh))
        causal = jnp.tril(jnp.ones((T, T), dtype=bool))
        att = jnp.where(causal[None, None], att, -jnp.inf)
        att = jax.nn.softmax(att, axis=-1)
        o = jnp.einsum('bhts,bhsd->bhtd', att, v)
        o = o.transpose(0, 2, 1, 3).reshape(B, T, N_EMBD)
        y = o @ Wo + bo
        mu = jnp.mean(y, axis=-1, keepdims=True)
        var = jnp.var(y, axis=-1, keepdims=True)
        return (y - mu) * jax.lax.rsqrt(var + EPS) * gamma + beta

    def _L0_ffn_ref(x, gate_w, gate_b, w1, b1, w2, b2, ln_g, ln_b):
        import jax, jax.numpy as jnp
        import numpy as np
        TOP_K = 2
        TEMP = 0.9
        EPS = 1e-05
        B, S, D, F, E = (2, 256, 128, 512, 8)

        def _moe_forward(x, gate_w, gate_b, w1, b1, w2, b2, ln_g, ln_b):
            logits = (x @ gate_w + gate_b) / TEMP
            topk_vals, topk_idx = jax.lax.top_k(logits, TOP_K)
            keep = jax.nn.one_hot(topk_idx, E, dtype=jnp.bool_).any(-2)
            masked = jnp.where(keep, logits, -jnp.inf)
            gate_probs = jax.nn.softmax(masked, axis=-1)
            h = jnp.einsum('bsd,edf->bsef', x, w1) + b1
            h = jax.nn.gelu(h, approximate=False)
            expert_out = jnp.einsum('bsef,efd->bsed', h, w2) + b2
            out = jnp.einsum('bse,bsed->bsd', gate_probs, expert_out)
            mu = out.mean(-1, keepdims=True)
            var = out.var(-1, keepdims=True)
            out = (out - mu) / jnp.sqrt(var + EPS) * ln_g + ln_b
            return out
        return _moe_forward(x, gate_w, gate_b, w1, b1, w2, b2, ln_g, ln_b)
    x = L0_attn_x
    mod = (_silu(L0_c) @ L0_wmod).reshape(L0_c.shape[0], 6, 1, -1)
    sa, ca, ga, sb, cb, gb = (mod[:, 0], mod[:, 1], mod[:, 2], mod[:, 3], mod[:, 4], mod[:, 5])
    ga = (2 * (ga >= 0) - 1) * jnp.maximum(jnp.abs(ga), 0.25)
    gb = (2 * (gb >= 0) - 1) * jnp.maximum(jnp.abs(gb), 0.25)
    h = _layernorm(x, axis=-1) * (1 + ca) + sa
    x = x + ga * _L0_attn_ref(h, L0_attn_Wq, L0_attn_bq, L0_attn_Wk, L0_attn_bk, L0_attn_Wv, L0_attn_bv, L0_attn_Wo, L0_attn_bo, L0_attn_gamma, L0_attn_beta)
    h = _layernorm(x, axis=-1) * (1 + cb) + sb
    x = x + gb * _L0_ffn_ref(h, L0_ffn_gate_w, L0_ffn_gate_b, L0_ffn_w1, L0_ffn_b1, L0_ffn_w2, L0_ffn_b2, L0_ffn_ln_g, L0_ffn_ln_b)
    return x

_drawn_inputs = setup_inputs


def setup_inputs(seed=0):
    import zlib

    import numpy as np

    out = dict(_drawn_inputs(seed))
    spreads = {'L0_attn_bq': (0.0, 0.8),
     'L0_attn_bk': (0.0, 0.8),
     'L0_attn_bv': (0.0, 0.1),
     'L0_attn_bo': (0.0, 0.1),
     'L0_attn_gamma': (1.0, 0.2),
     'L0_attn_beta': (0.0, 0.1),
     'L0_ffn_gate_b': (0.0, 0.1),
     'L0_ffn_b1': (0.0, 0.32),
     'L0_ffn_b2': (0.0, 0.1),
     'L0_ffn_ln_g': (1.0, 0.2),
     'L0_ffn_ln_b': (0.0, 0.364)}
    factors = {'L0_attn_Wq': 8.0, 'L0_attn_Wk': 7.488}
    for name, (base, spread) in spreads.items():
        noise = np.random.default_rng([zlib.crc32(name.encode()), seed]).standard_normal(out[name].shape)
        drawn = base * np.exp(spread * noise) if base else spread * noise
        out[name] = jnp.asarray(drawn.astype(out[name].dtype))
    for name, factor in factors.items():
        out[name] = (out[name] * factor).astype(out[name].dtype)
    return out
```

```python
from contextlib import ExitStack

import concourse.bass as bass
from concourse import mybir

F32 = mybir.dt.float32
F32R = mybir.dt.float32r
ALU = mybir.AluOpType
ACT = mybir.ActivationFunctionType
AX = mybir.AxisListType

P = 128
EPS = 1e-5
TEMP = 0.9
LOWEST = -3.0e38


def ds(i, n=1):
    return bass.ds(i, n)


def build(nc, x, wq, bq, wk, bk, wv, bv, wo, bo, gamma, beta, gate_w, gate_b, w1, b1, w2, b2,
          ln_g, ln_b, c, wmod, out):
    B, T, C = x.shape
    H, DH = 16, C // 16
    E, _, F = w1.shape
    TT = T // P
    NT = B * TT
    QUADS = H // 4
    FC = F // P
    N = B * T
    assert C == P and T == 512 and DH == 8 and FC == 4
    SCALE = float(DH) ** -0.5

    ROW_BQ, ROW_BK, ROW_C, NROWS = E * FC, E * FC + 1, E * FC + 2, E * FC + 2 + B

    Q_PIECE, K_PIECE = (0, 0, 1), (0, 1, 0)
    MAX_ROW = 3 * DH
    ROWS = MAX_ROW + 2
    ONE = 1

    FILLS = [[(0, 3, 0)], [(1, 3, 0)], [(0, 2, 0), (0, 0, 384)], [(1, 2, 0), (1, 0, 384)],
             [(2, 3, 0)], [(3, 3, 0)], [(2, 2, 0), (2, 0, 384)], [(3, 2, 0), (3, 0, 384)],
             [(0, 1, 0), (2, 1, 256)], [(1, 1, 0), (3, 1, 256)]]
    NFILL = len(FILLS)
    AFTER = []
    for f in range(NFILL):
        AFTER.append((AFTER[-1] if AFTER else 0) + len(FILLS[f]))
    NMAX = AFTER[-1]
    UNITS = [[(0, 0, 0), (1, 0, 512)], [(2, 0, 0), (3, 0, 512)],
             [(0, 3, 0), (0, 1, 128), (1, 3, 512), (1, 1, 640)],
             [(2, 3, 0), (2, 1, 128), (3, 3, 512), (3, 1, 640)],
             [(0, 2, 0), (2, 2, 256), (1, 2, 512), (3, 2, 768)]]
    NU = len(UNITS)
    PLACE = {(h, ch): u * 1024 + col for u, parts in enumerate(UNITS) for h, ch, col in parts}
    PV_ORDER = [(0, 1), (1, 3), (3, 3), (2, 4)]

    q_rows = nc.dram_tensor("q_rows", [B, H, ROWS, T], F32)
    k_rows = nc.dram_tensor("k_rows", [B, H, ROWS, T], F32)
    gates_dram = nc.dram_tensor("gates_dram", [E, N], F32)

    x_v = x.rearrange("b (t p) c -> p (b t) c", p=P)
    out_v = out.rearrange("b (t p) c -> p (b t) c", p=P)
    w1_v = w1.rearrange("e d f -> d e f")
    w2_v = w2.rearrange("e (k f) d -> f e k d", f=P)

    def row(v):
        return v.rearrange("(o n) -> o n", o=1).to_broadcast([P, v.shape[0]])

    with ExitStack() as whole:
        def sem(name):
            return whole.enter_context(nc.semaphore(name))

        def shared(name, shape, dt=F32):
            return whole.enter_context(nc.sbuf_tensor(name, shape, dt))

        xs = shared("xs", [P, NT, C])
        ident = shared("ident", [P, P])
        cols = shared("cols", [P, NROWS])
        half_neg = shared("half_neg", [P, NT])
        gate_out = shared("gate_out", [P, B, C])
        bias_out = shared("bias_out", [P, B, C])
        h2_hi = shared("h2_hi", [P, N], F32R)
        h2_lo = shared("h2_lo", [P, N], F32R)
        logits = shared("logits", [P, NT, E])
        gate_b_all = shared("gate_b_all", [P, E])
        w1_raw = shared("w1_raw", [P, 2, F])
        w2_raw = shared("w2_raw", [P, 2, FC, C])
        b2_rows = shared("b2_rows", [E, C])

        w_in = sem("w_in")
        go = sem("go")

        def wait_apart(eng, sem_, value):
            if not isinstance(value, int):
                value = eng.to_reg(value)
                eng.wait_ge(go, 1)
            eng.wait_ge(sem_, value)

        with ExitStack() as ctx:
            def sb(name, shape, dt=F32):
                return ctx.enter_context(nc.sbuf_tensor(name, shape, dt))

            def ps(name, shape):
                return ctx.enter_context(nc.psum_tensor(name, shape, F32))

            mask = sb("mask", [P, T])
            rows = sb("rows", [NROWS, P])
            wqs, wks, wvs, wos = (sb(n, [P, C]) for n in ("wqs", "wks", "wvs", "wos"))
            gws = sb("gws", [P, E])
            wmods = sb("wmods", [P, 6 * C])
            bv_all, bo_all, gam_all, bet_all, lng_all, lnb_all = (
                sb(n, [P, C]) for n in ("bv_all", "bo_all", "gam_all", "bet_all", "lng_all", "lnb_all"))
            sil = sb("sil", [P, 3, B])
            silu = sb("silu", [P, B])
            silu_wide = sb("silu_wide", [P, B, P])
            modc = sb("modc", [P, 4, B])
            gate_mid = sb("gate_mid", [P, B, C])
            bias_mid = sb("bias_mid", [P, B, C])
            stats = sb("stats", [P, TT, 6])
            mv = sb("mv", [P, TT, 2])
            vare = sb("vare", [P, TT])
            rstd = sb("rstd", [P, TT])
            norm = sb("norm", [P, TT, C])
            hT = sb("hT", [P, T])
            q_out = sb("q_out", [P, 2, T], F32R)
            k_out = sb("k_out", [P, 2, T], F32R)
            v_all = sb("v_all", [P, B, TT, C])
            v_pad = sb("v_pad", [P, TT, H, 32])
            qa = sb("qa", [P, 2, 2, T], F32R)
            ka = sb("ka", [P, 2, 2, T], F32R)
            qb = sb("qb", [P, QUADS, 2, T], F32R)
            kb = sb("kb", [P, QUADS, 2, T], F32R)
            junk = sb("junk", [P, 2, T])
            maxes = sb("maxes", [P, H * TT])
            max_out = sb("max_out", [4 * TT, QUADS, 2, P], F32R)
            probs = sb("probs", [P, 2, NU * 1024])
            clamp = probs[:, 0, 0:8 * B * C].rearrange("p (n b c) -> p n b c", b=B, c=C)
            o_spread = sb("o_spread", [P, QUADS, T])
            ones = junk[0:B * H]
            rec = sb("rec", [P, TT, H])
            o_norm = sb("o_norm", [P, TT, C])
            oT = sb("oT", [P, T])
            ys = sb("ys", [P, TT, C])
            h2 = sb("h2", [P, T])

            S = ps("S", [P, 2, 1024])
            X = ps("X", [P, 2, 512])
            O = ps("O", [P, 512])
            M = ps("M", [P, 512])

            rows_in, mod_in, proj_in, bcast_in, late_in = map(sem, ("rows_in", "mod_in", "proj_in", "bcast_in", "late_in"))
            x_in, ones_saved = sem("x_in"), sem("ones_saved")
            ident_set, consts_set, zero_set = map(sem, ("ident_set", "consts_set", "zero_set"))
            cols_ps, cols_set = sem("cols_ps"), sem("cols_set")
            sil_exp, sil_step = sem("sil_exp"), sem("sil_step")
            mod_ps, gmid_ps, gout_ps, modc_set, clamped, modrow_set = map(sem, ("mod_ps", "gmid_ps", "gout_ps", "modc_set", "clamped", "modrow_set"))
            x_stat, x_aggr, x_var, x_rstd, x_norm = map(sem, ("x_stat", "x_aggr", "x_var", "x_rstd", "x_norm"))
            xT_ps, hT_set, q_ps, k_ps, v_ps = map(sem, ("xT_ps", "hT_set", "q_ps", "k_ps", "v_ps"))
            q_hi, q_lo, k_hi, k_lo, v_set, qk_saved = map(sem, ("q_hi", "q_lo", "k_hi", "k_lo", "v_set", "qk_saved"))
            a_in = [sem(f"a_in{s}") for s in range(2)]
            b_in = [sem(f"b_in{q}") for q in range(QUADS)]
            fill_ps, rowmax, maxT_ps, max_hi, max_lo, max_saved = map(sem, ("fill_ps", "rowmax", "maxT_ps", "max_hi", "max_lo", "max_saved"))
            vpad_set, unit_ps, exps, masked, pv_ps, o_out = map(sem, ("vpad_set", "unit_ps", "exps", "masked", "pv_ps", "o_out"))
            oT1_ps, rec_set, onorm_set, oT2_ps, oT_set, y_ps, y_set = map(sem, ("oT1_ps", "rec_set", "onorm_set", "oT2_ps", "oT_set", "y_ps", "y_set"))
            y_stat, y_aggr, y_var, y_rstd, y_norm, y_gated, xb_set, x1_set = map(sem, ("y_stat", "y_aggr", "y_var", "y_rstd", "y_norm", "y_gated", "xb_set", "x1_set"))
            r_stat, r_aggr, r_var, r_rstd, r_norm, rT_ps = map(sem, ("r_stat", "r_aggr", "r_var", "r_rstd", "r_norm", "rT_ps"))
            h2hi_set, h2_set, h2lo_set, lg_ps, lg_set = map(sem, ("h2hi_set", "h2_set", "h2lo_set", "lg_ps", "lg_set"))

            from_one = (x_in, hT_set, q_lo, k_lo, v_set, v_ps, qk_saved, x_norm, xT_ps,
                        exps, h2hi_set, h2_set, lg_set, o_out, oT1_ps, pv_ps, y_ps, oT2_ps, lg_ps, max_saved)

            block = ctx.enter_context(nc.Block())

            @block.sync
            def _(sp):
                sp.wait_ge(go, 1)
                sp.dma_start(rows[0:E * FC, :], b1.rearrange("e (k f) -> (e k) f", f=P)).then_inc(rows_in, 16)
                sp.dma_start(rows[ROW_BQ:ROW_BQ + 1, :], bq.rearrange("(o n) -> o n", o=1)).then_inc(rows_in, 16)
                sp.dma_start(rows[ROW_BK:ROW_BK + 1, :], bk.rearrange("(o n) -> o n", o=1)).then_inc(rows_in, 16)
                sp.dma_start(rows[ROW_C:NROWS, :], c).then_inc(rows_in, 16)
                sp.dma_start(wmods[:], wmod).then_inc(mod_in, 16)
                with sp.Fori(0, B) as b:
                    sp.wait_ge(x_in, ONE + 16 * b)
                    sp.dma_start(xs[:, ds(TT * b, TT), :], x_v[:, ds(TT * b, TT), :]).then_inc(x_in, 16)
                for dst, src in ((wqs, wq), (wks, wk), (wvs, wv)):
                    sp.dma_start(dst[:], src).then_inc(proj_in, 16)
                for dst, src in ((bv_all, bv), (gam_all, gamma), (bet_all, beta), (lng_all, ln_g), (lnb_all, ln_b)):
                    sp.dma_start(dst[:], row(src)).then_inc(bcast_in, 16)
                for dst, src in ((bo_all, row(bo)), (gate_b_all, row(gate_b)), (wos, wo), (gws, gate_w), (b2_rows, b2)):
                    sp.dma_start(dst[:], src).then_inc(late_in, 16)
                sp.dma_start(w1_raw[:], w1_v[:, 0:2, :]).then_inc(w_in, 16)
                sp.dma_start(w2_raw[:], w2_v[:, 0:2, :, :]).then_inc(w_in, 16)

                sp.wait_ge(zero_set, 5)
                sp.dma_start(k_rows[:, :, MAX_ROW:ROWS, :].rearrange("b h r t -> (b h) (r t)"),
                             ones[:].rearrange("p r t -> p (r t)")).then_inc(ones_saved, 16)
                with sp.Fori(0, B) as b:
                    for done, src, dst, piece in ((q_lo, q_out, q_rows, Q_PIECE), (k_lo, k_out, k_rows, K_PIECE)):
                        sp.wait_ge(done, ONE + b + 1)
                        rows_of = dst[ds(b)].rearrange("o h r t -> (o h) r t")
                        for r, half in enumerate(piece):
                            sp.dma_start(rows_of[:, DH * r:DH * (r + 1), :], src[:, half, :].bitcast(F32)).then_inc(qk_saved, 16)

                def load_a(b, q):
                    if not (isinstance(b, int) and b == 0 and q < 2):
                        sp.wait_ge(maxT_ps, QUADS * b + q - 1)
                    for dst, src in ((qa, q_rows), (ka, k_rows)):
                        heads = src[ds(b)].rearrange("o (g par) r t -> (o par) r g t", par=2)
                        for par in range(2):
                            sp.dma_start(dst[64 * par:64 * par + MAX_ROW, q % 2].bitcast(F32),
                                         heads[par, 0:MAX_ROW, 2 * q:2 * q + 2, :]).then_inc(a_in[q % 2], 16)

                def load_b(b, q):
                    if not (isinstance(b, int) and b == 0):
                        sp.wait_ge(unit_ps, NU * (QUADS * (b - 1) + q + 1))
                    for dst, src in ((kb, k_rows), (qb, q_rows)):
                        heads = src[ds(b)].rearrange("o (g par) r t -> (o par) r g t", par=2)
                        if dst is qb:
                            sp.wait_ge(max_lo, QUADS * b + q + 1)
                            for half in range(2):
                                sp.dma_start(src[ds(b), 4 * q:4 * q + 4, MAX_ROW + half].rearrange("o h (t p) -> (o h) t p", p=P),
                                             max_out[:, q, half, :].bitcast(F32)).then_inc(max_saved, 16)
                            sp.wait_ge(max_saved, ONE + 32 * (QUADS * b + q + 1))
                        for par in range(2):
                            sp.dma_start(dst[64 * par:64 * par + ROWS, q].bitcast(F32),
                                         heads[par, :, 2 * q:2 * q + 2, :]).then_inc(b_in[q], 16)

                def stage(b):
                    load_a(b, 0)
                    load_a(b, 1)
                    for q in range(QUADS):
                        load_b(b, q)
                        if q + 2 < QUADS:
                            load_a(b, q + 2)

                sp.wait_ge(ones_saved, 16)
                sp.wait_ge(qk_saved, ONE + 96 * B)
                stage(0)
                with sp.Fori(0, B - 1) as b:
                    stage(b + 1)

            @block.gpsimd
            def _(pool):
                pool.memset(ident[:], 0.0).then_inc(ident_set, 1)
                for s_ in from_one:
                    pool.sem_inc(s_, ONE)
                pool.sem_inc(go, 1)
                pool.wait_ge(ident_set, 1)
                pool.affine_select(out=ident[:], in_=ident[:], compare_op=ALU.not_equal, fill=1.0, base=0,
                                   pattern=[[-1, P]], channel_multiplier=1).then_inc(ident_set, 1)
                pool.memset(half_neg[:], -0.5).then_inc(consts_set, 1)
                pool.memset(mask[:], 0.0).then_inc(consts_set, 1)
                pool.wait_ge(consts_set, 2)
                pool.affine_select(out=mask[:, T - P:T], in_=mask[:, T - P:T], compare_op=ALU.is_ge, fill=LOWEST, base=0,
                                   pattern=[[-1, P]], channel_multiplier=1).then_inc(consts_set, 1)
                pool.memset(v_pad[:], 0.0).then_inc(consts_set, 1)
                pool.memset(kb[:].bitcast(F32), 0.0).then_inc(zero_set, 1)
                pool.memset(qb[:].bitcast(F32), 0.0).then_inc(zero_set, 1)
                pool.wait_ge(consts_set, 4)
                pool.memset(v_pad[:, :, :, DH:DH + 1], 1.0).then_inc(consts_set, 1)

                def inv_sqrt(var, done, b):
                    pool.wait_ge(var, b + 1)
                    pool.tensor_tensor(rstd[:], vare[:], half_neg[:, 0:TT], ALU.pow).then_inc(done, 1)

                with pool.Fori(0, B) as b:
                    inv_sqrt(x_var, x_rstd, b)

                def attend(b):
                    for q in range(QUADS):
                        for u in range(NU):
                            wait_apart(pool, exps, ONE + NU * (QUADS * b + q) + u + 1)
                            if u < 2:
                                v = probs[:, q % 2, ds(u * 1024, 1024)].rearrange("p (h c) -> p h c", h=2)[:, :, 0:P]
                                pattern = [[0, 2], [1, P]]
                            elif u < 4:
                                v = probs[:, q % 2, ds(u * 1024, 1024)].rearrange("p (h c) -> p h c", h=2)[:, :, 0:2 * P]
                                pattern = [[0, 2], [0, 2], [1, P]]
                            else:
                                v = probs[:, q % 2, ds(u * 1024, 1024)].rearrange("p (h c) -> p h c", h=4)[:, :, 0:P]
                                pattern = [[0, 4], [1, P]]
                            pool.affine_select(out=v, in_=v, compare_op=ALU.is_ge, fill=0.0, base=0,
                                               pattern=pattern, channel_multiplier=-1).then_inc(masked, 1)

                def finish(b):
                    pool.tensor_tensor(xs[:, ds(TT * b, TT), :], xs[:, ds(TT * b, TT), :],
                                       bias_mid[:, ds(b), :].to_broadcast([P, TT, C]), ALU.add).then_inc(xb_set, 1)
                    inv_sqrt(y_var, y_rstd, b)
                    inv_sqrt(r_var, r_rstd, b)

                pool.wait_ge(modrow_set, 4)
                pool.wait_ge(x_norm, ONE + NT)
                with pool.Fori(0, B - 1) as b:
                    attend(b)
                    finish(b)
                attend(B - 1)
                finish(B - 1)

            @block.tensor
            def _(pe):
                pe.wait_ge(go, 1)
                pe.wait_ge(ident_set, 2)
                pe.wait_ge(rows_in, 64)
                pe.transpose(M[:, 0:NROWS], rows[:], ident[0:NROWS, 0:NROWS]).then_inc(cols_ps, 1)
                pe.wait_ge(sil_step, 4)
                pe.wait_ge(mod_in, 16)
                for n, j in enumerate((0, 1, 3, 4)):
                    mm = pe.matmul(O[:, n * B:(n + 1) * B], wmods[:, j * C:(j + 1) * C], silu[:], start=True, stop=True)
                mm.then_inc(mod_ps, 1)
                for j, bank, done in ((2, 0, gmid_ps), (5, 1, gout_ps)):
                    for b in range(B):
                        mm = pe.matmul(S[:, 0, ds(bank * 512 + b * C, C)], silu_wide[:, b, :], wmods[:, j * C:(j + 1) * C],
                                       start=True, stop=True)
                    mm.then_inc(done, 1)
                pe.wait_ge(proj_in, 48)
                pe.wait_ge(cols_set, 1)
                pe.wait_ge(modc_set, 2)

                with pe.Fori(0, B) as b:
                    pe.wait_ge(x_norm, ONE + TT * b + TT)
                    pe.wait_ge(hT_set, ONE + b)
                    for t in range(TT):
                        mm = pe.transpose(M[:, t * P:(t + 1) * P], norm[:, t, :], ident[:])
                    mm.then_inc(xT_ps, 1)
                    pe.wait_ge(hT_set, ONE + b + 1)
                    pe.wait_ge(q_lo, ONE + b)
                    pe.matmul(O[:], wqs[:], hT[:], start=True, stop=True).then_inc(q_ps, 1)
                    pe.wait_ge(k_lo, ONE + b)
                    pe.matmul(X[:, 0, :], wks[:], hT[:], start=True, stop=True).then_inc(k_ps, 1)
                    pe.wait_ge(v_set, ONE + b)
                    for t in range(TT):
                        mm = pe.matmul(X[:, 1, t * C:(t + 1) * C], hT[:, t * P:(t + 1) * P], wvs[:], start=True, stop=True)
                    mm.then_inc(v_ps, 1)

                def rowmax_fill(b, q, f):
                    if f == 0:
                        pe.wait_ge(a_in[q % 2], 64 * (2 * b + q // 2 + 1))
                    if not (isinstance(b, int) and b == 0 and q == 0 and f < 2):
                        before = AFTER[f - 2] if f >= 2 else AFTER[f - 2] - NMAX
                        pe.wait_ge(rowmax, NMAX * (QUADS * b + q) + before)
                    for head, tile, col in FILLS[f]:
                        pair, rows_ = head // 2, slice(64 * (head % 2), 64 * (head % 2) + 64)
                        mm = pe.matmul(X[:, f % 2, col:col + P * (tile + 1)], qa[rows_, q % 2, pair, tile * P:(tile + 1) * P],
                                       ka[rows_, q % 2, pair, 0:P * (tile + 1)], start=True, stop=True, skip_group_check=True)
                    mm.then_inc(fill_ps, 1)

                def max_turn(b, q):
                    pe.wait_ge(rowmax, NMAX * (QUADS * b + q + 1))
                    pe.wait_ge(max_lo, QUADS * b + q)
                    if q == 0 and not (isinstance(b, int) and b == 0):
                        pe.wait_ge(h2hi_set, ONE + b - 1)
                        pe.wait_ge(h2_set, ONE + b - 1)
                    pe.transpose(M[0:4 * TT, 0:P], maxes[:, 4 * TT * q:4 * TT * (q + 1)], ident[:]).then_inc(maxT_ps, 1)

                def scores(b, q, u):
                    if u == 0:
                        pe.wait_ge(b_in[q], 64 * (b + 1))
                    pe.wait_ge(exps, ONE + NU * QUADS * b + max(NU * q + u - 1, 0))
                    slot = (NU * q + u) % 2
                    for head, ch, col in UNITS[u]:
                        rows_ = slice(64 * (head % 2), 64 * (head % 2) + 64)
                        mm = pe.matmul(S[:, slot, col:col + T - P * ch], kb[rows_, q, head // 2, ch * P:(ch + 1) * P],
                                       qb[rows_, q, head // 2, ch * P:T], start=True, stop=True, skip_group_check=True)
                    mm.then_inc(unit_ps, 1)

                def values(b, q, n):
                    ch, unit = PV_ORDER[n]
                    if n == 0:
                        if q == 0:
                            pe.wait_ge(vpad_set, b + 1)
                            pe.wait_ge(lg_set, ONE + b)
                        pe.wait_ge(o_out, ONE + QUADS * b + q)
                    pe.wait_ge(masked, NU * (QUADS * b + q) + unit + 1)
                    for j in range(4):
                        at = PLACE[j, ch]
                        mm = pe.matmul(O[32 * j:32 * j + 32, ch * P:T], v_pad[:, ch, 4 * q + j, :],
                                       probs[:, q % 2, at:at + T - P * ch], start=(n == 0), stop=(n == TT - 1),
                                       tile_position=(0, 32 * j), skip_group_check=True)
                    if n == TT - 1:
                        mm.then_inc(pv_ps, 1)

                def attend(b, nxt):
                    for q in range(QUADS):
                        for s in range(NFILL):
                            if s % 2 == 0:
                                scores(b, q, s // 2)
                            if nxt is not None:
                                rowmax_fill(nxt, q, s)
                                if s == 1 and q >= 1:
                                    max_turn(nxt, q - 1)
                            if s % 2 == 1 and s < 9 and q >= 1:
                                values(b, q - 1, s // 2)
                    if nxt is not None:
                        max_turn(nxt, QUADS - 1)
                    for n in range(TT):
                        values(b, QUADS - 1, n)

                def finish(b, nxt):
                    pe.wait_ge(o_out, ONE + QUADS * b + QUADS)
                    if nxt is not None:
                        pe.wait_ge(max_lo, QUADS * nxt + QUADS)
                    for t in range(TT):
                        bank = (M, O)[t % 2]
                        if t >= 2:
                            pe.wait_ge(onorm_set, TT * b + t - 1)
                        for q in range(QUADS):
                            mm = pe.transpose(bank[:, q * P:(q + 1) * P], o_spread[:, q, t * P:(t + 1) * P], ident[:])
                        mm.then_inc(oT1_ps, 1)
                    for t in range(TT):
                        pe.wait_ge(onorm_set, TT * b + max(t, 2) + 1)
                        mm = pe.transpose(M[:, t * P:(t + 1) * P], o_norm[:, t, :], ident[:])
                    mm.then_inc(oT2_ps, 1)
                    pe.wait_ge(oT_set, b + 1)
                    for t in range(TT):
                        mm = pe.matmul(O[:, t * C:(t + 1) * C], oT[:, t * P:(t + 1) * P], wos[:], start=True, stop=True)
                    mm.then_inc(y_ps, 1)
                    for t in range(TT):
                        pe.wait_ge(r_norm, TT * b + t + 1)
                        mm = pe.transpose(M[:, t * P:(t + 1) * P], norm[:, t, :], ident[:])
                    mm.then_inc(rT_ps, 1)
                    pe.wait_ge(h2_set, ONE + b + 1)
                    for t in range(TT):
                        mm = pe.matmul(O[:, t * E:(t + 1) * E], h2[:, t * P:(t + 1) * P], gws[:], start=True, stop=True)
                    mm.then_inc(lg_ps, 1)

                pe.wait_ge(q_lo, ONE + B)
                pe.wait_ge(k_lo, ONE + B)
                pe.wait_ge(v_set, ONE + B)
                pe.wait_ge(clamped, 8)
                pe.wait_ge(consts_set, 5)
                pe.wait_ge(late_in, 80)
                for q in range(QUADS):
                    for f in range(NFILL):
                        rowmax_fill(0, q, f)
                    max_turn(0, q)
                with pe.Fori(0, B - 1) as b:
                    attend(b, b + 1)
                    finish(b, b + 1)
                attend(B - 1, None)
                finish(B - 1, None)

            @block.scalar
            def _(act):
                act.wait_ge(go, 1)
                act.wait_ge(cols_ps, 1)
                act.activation(cols[:], M[:, 0:NROWS], ACT.Copy).then_inc(cols_set, 1)
                act.wait_ge(cols_set, 1)
                act.activation(sil[:, 0, :], cols[:, ROW_C:ROW_C + B], ACT.Exp, scale=-1.0).then_inc(sil_exp, 1)

                with act.Fori(0, B) as b:
                    act.wait_ge(modc_set, 2)
                    wait_apart(act, xT_ps, ONE + b + 1)
                    wait_apart(act, v_ps, ONE + b)
                    act.activation(hT[:], M[:], ACT.Identity, scale=modc[:, 1, ds(b)], bias=modc[:, 0, ds(b)]).then_inc(hT_set, 1)
                    act.wait_ge(qk_saved, ONE + 96 * b)
                    act.wait_ge(q_ps, b + 1)
                    act.activation(q_out[:, 0, :], O[:], ACT.Identity, bias=cols[:, ROW_BQ:ROW_BQ + 1]).then_inc(q_hi, 1)
                    act.wait_ge(k_ps, b + 1)
                    act.activation(k_out[:, 0, :], X[:, 0, :], ACT.Identity, bias=cols[:, ROW_BK:ROW_BK + 1]).then_inc(k_hi, 1)

                def o_copy(b, q):
                    act.wait_ge(pv_ps, ONE + QUADS * b + q + 1)
                    if q == 0:
                        act.wait_ge(oT1_ps, ONE + TT * b)
                    act.activation(o_spread[:, q, :], O[:], ACT.Copy).then_inc(o_out, 1)

                def attend(b):
                    wait_apart(act, pv_ps, ONE + QUADS * b)
                    act.activation(v_pad[:, :, :, 0:DH], v_all[:, ds(b), :, :].rearrange("p o t (h i) -> p (o t) h i", i=DH),
                                   ACT.Copy).then_inc(vpad_set, 1)
                    for q in range(QUADS):
                        if q >= 2:
                            act.wait_ge(pv_ps, ONE + QUADS * b + q - 1)
                        for u in range(NU):
                            act.wait_ge(unit_ps, NU * (QUADS * b + q) + u + 1)
                            act.activation(probs[:, q % 2, u * 1024:(u + 1) * 1024], S[:, (NU * q + u) % 2, :],
                                           ACT.Exp, scale=SCALE).then_inc(exps, 1)
                        if q >= 1:
                            o_copy(b, q - 1)
                    o_copy(b, QUADS - 1)

                def finish(b):
                    act.wait_ge(oT2_ps, ONE + b + 1)
                    act.wait_ge(y_ps, ONE + b)
                    act.activation(oT[:], M[:], ACT.Copy).then_inc(oT_set, 1)
                    wait_apart(act, rT_ps, b + 1)
                    act.activation(h2_hi[:, ds(T * b, T)], M[:], ACT.Identity, scale=modc[:, 3, ds(b)],
                                   bias=modc[:, 2, ds(b)]).then_inc(h2hi_set, 1)

                act.wait_ge(v_set, ONE + B)
                act.wait_ge(consts_set, 5)
                with act.Fori(0, B - 1) as b:
                    attend(b)
                    finish(b)
                attend(B - 1)
                finish(B - 1)

            @block.vector
            def _(dve):
                dve.wait_ge(go, 1)
                dve.memset(ones, 1.0).then_inc(zero_set, 1)
                dve.memset(qa[:].bitcast(F32), 0.0).then_inc(zero_set, 1)
                dve.memset(ka[:].bitcast(F32), 0.0).then_inc(zero_set, 1)
                dve.wait_ge(sil_exp, 1)
                dve.tensor_scalar(sil[:, 1, :], sil[:, 0, :], 1.0, None, ALU.add).then_inc(sil_step, 1)
                dve.wait_ge(sil_step, 1)
                dve.reciprocal(sil[:, 2, :], sil[:, 1, :]).then_inc(sil_step, 1)
                dve.wait_ge(sil_step, 2)
                dve.tensor_tensor(silu[:], cols[:, ROW_C:ROW_C + B], sil[:, 2, :], ALU.mult).then_inc(sil_step, 1)
                dve.wait_ge(sil_step, 3)
                dve.tensor_copy(silu_wide[:], silu[:].unsqueeze(2).to_broadcast([P, B, P])).then_inc(sil_step, 1)
                dve.wait_ge(mod_ps, 1)
                mods = O[:, 0:4 * B].rearrange("p (n b) -> p n b", b=B)
                dve.tensor_copy(modc[:, 0:4:2, :], mods[:, 0:4:2, :]).then_inc(modc_set, 1)
                dve.tensor_scalar(modc[:, 1:4:2, :], mods[:, 1:4:2, :], 1.0, None, ALU.add).then_inc(modc_set, 1)

                def layer_stats(src, stat, aggr, var, b):
                    for t in range(TT):
                        dve.bn_stats(stats[:, t, :], src(t)).then_inc(stat, 1)
                    for t in range(TT):
                        wait_apart(dve, stat, TT * b + t + 1)
                        dve.bn_aggr(mv[:, t, :], stats[:, t, :]).then_inc(aggr, 1)
                    dve.wait_ge(aggr, TT * b + TT)
                    dve.tensor_scalar(vare[:], mv[:, :, 1], EPS, None, ALU.add).then_inc(var, 1)

                def normalise(src, dst, rs, done, b):
                    dve.wait_ge(rs, b + 1)
                    for t in range(TT):
                        dve.tensor_scalar(dst[:, t, :], src(t), mv[:, t, 0:1], rstd[:, t:t + 1],
                                          ALU.subtract, ALU.mult).then_inc(done, 1)

                def tile_of_x(b):
                    return lambda t: xs[:, ds(TT * b + t), :].rearrange("p o c -> p (o c)")

                def x_stats(b):
                    dve.wait_ge(x_in, ONE + 16 * b + 16)
                    wait_apart(dve, x_norm, ONE + TT * b)
                    layer_stats(tile_of_x(b), x_stat, x_aggr, x_var, b)

                def project(b, nxt):
                    dve.wait_ge(xT_ps, ONE + b)
                    normalise(tile_of_x(b), norm, x_rstd, x_norm, b)
                    if nxt is not None:
                        x_stats(nxt)
                    dve.wait_ge(q_hi, b + 1)
                    dve.scalar_tensor_tensor(out=q_out[:, 1, :], in0=O[:], scalar=cols[:, ROW_BQ:ROW_BQ + 1],
                                             in1=q_out[:, 0, :].bitcast(F32), op0=ALU.add, op1=ALU.subtract).then_inc(q_lo, 1)
                    dve.wait_ge(k_hi, b + 1)
                    dve.scalar_tensor_tensor(out=k_out[:, 1, :], in0=X[:, 0, :], scalar=cols[:, ROW_BK:ROW_BK + 1],
                                             in1=k_out[:, 0, :].bitcast(F32), op0=ALU.add, op1=ALU.subtract).then_inc(k_lo, 1)
                    dve.wait_ge(v_ps, ONE + b + 1)
                    dve.wait_ge(bcast_in, 80)
                    dve.tensor_tensor(v_all[:, ds(b), :, :].rearrange("p o t c -> p (o t) c"),
                                      X[:, 1, :].rearrange("p (t c) -> p t c", c=C),
                                      bv_all[:].unsqueeze(1).to_broadcast([P, TT, C]), ALU.add).then_inc(v_set, 1)

                x_stats(0)
                with dve.Fori(0, B - 1) as b:
                    project(b, b + 1)
                project(B - 1, None)

                for n, (done, bank, wt, bs, g_dst, b_dst) in enumerate((
                        (gmid_ps, 0, gam_all, bet_all, gate_mid, bias_mid),
                        (gout_ps, 1, lng_all, lnb_all, gate_out, bias_out))):
                    g = S[:, 0, bank * 512:bank * 512 + 512].rearrange("p (b c) -> p b c", c=C)
                    dve.wait_ge(done, 1)
                    twice, sign, size, signed = (clamp[:, 4 * n + k] for k in range(4))
                    dve.tensor_scalar(twice, g, 0.0, 2.0, ALU.is_ge, ALU.mult).then_inc(clamped, 1)
                    dve.wait_ge(clamped, 4 * n + 1)
                    dve.tensor_scalar(sign, twice, -1.0, None, ALU.add).then_inc(clamped, 1)
                    dve.scalar_tensor_tensor(out=size, in0=twice, scalar=-1.0, in1=g, op0=ALU.add, op1=ALU.mult).then_inc(clamped, 1)
                    dve.wait_ge(clamped, 4 * n + 3)
                    dve.scalar_tensor_tensor(out=signed, in0=size, scalar=0.25, in1=sign, op0=ALU.max, op1=ALU.mult).then_inc(clamped, 1)
                    dve.wait_ge(clamped, 4 * n + 4)
                    dve.tensor_tensor(g_dst[:], signed, wt[:].unsqueeze(1).to_broadcast([P, B, C]), ALU.mult).then_inc(modrow_set, 1)
                    dve.tensor_tensor(b_dst[:], signed, bs[:].unsqueeze(1).to_broadcast([P, B, C]), ALU.mult).then_inc(modrow_set, 1)

                def max_fill(b, q, f):
                    wait_apart(dve, fill_ps, NFILL * (QUADS * b + q) + f + 1)
                    k = AFTER[f] - len(FILLS[f])
                    for n, (head, tile, col) in enumerate(FILLS[f]):
                        if not (isinstance(b, int) and b == 0 and q == 0 and k + n < 2):
                            wait_apart(dve, rowmax, NMAX * (QUADS * b + q) + k + n - 1)
                        width = P * (tile + 1)
                        at = TT * (4 * q + head) + tile
                        dve.tensor_tensor_reduce(out=junk[:, (k + n) % 2, 0:width], in0=X[:, f % 2, col:col + width],
                                                 in1=mask[:, T - width:T], scale=1.0, scalar=LOWEST, op0=ALU.add,
                                                 op1=ALU.max, accum_out=maxes[:, at:at + 1]).then_inc(rowmax, 1)

                def max_split(b, q):
                    dve.wait_ge(maxT_ps, QUADS * b + q + 1)
                    dve.wait_ge(max_saved, ONE + 32 * QUADS * b)
                    turned = M[0:4 * TT, 0:P]
                    dve.tensor_scalar(max_out[:, q, 0, :], turned, -1.0, None, ALU.mult).then_inc(max_hi, 1)
                    dve.wait_ge(max_hi, QUADS * b + q + 1)
                    dve.scalar_tensor_tensor(out=max_out[:, q, 1, :], in0=turned, scalar=-1.0, in1=max_out[:, q, 0, :].bitcast(F32),
                                             op0=ALU.mult, op1=ALU.subtract).then_inc(max_lo, 1)

                def row_maxima(b):
                    for q in range(QUADS):
                        for f in range(NFILL):
                            max_fill(b, q, f)
                            if f == 1 and q >= 1:
                                max_split(b, q - 1)
                    max_split(b, QUADS - 1)

                def finish(b):
                    for t in range(TT):
                        dve.wait_ge(oT1_ps, ONE + TT * b + t + 1)
                        o = (M, O)[t % 2][:].rearrange("p (h i) -> p h i", i=32)
                        dve.reciprocal(rec[:, t, :], o[:, :, DH]).then_inc(rec_set, 1)
                        dve.wait_ge(rec_set, TT * b + t + 1)
                        dve.wait_ge(oT2_ps, ONE + b)
                        dve.tensor_tensor(o_norm[:, t, :].rearrange("p (h i) -> p h i", i=DH), o[:, :, 0:DH],
                                          rec[:, t, :].unsqueeze(2).to_broadcast([P, H, DH]), ALU.mult).then_inc(onorm_set, 1)
                    dve.wait_ge(y_ps, ONE + b + 1)
                    dve.tensor_tensor(ys[:], O[:].rearrange("p (t c) -> p t c", c=C),
                                      bo_all[:].unsqueeze(1).to_broadcast([P, TT, C]), ALU.add).then_inc(y_set, 1)
                    wait_apart(dve, y_set, b + 1)
                    layer_stats(lambda t: ys[:, t, :], y_stat, y_aggr, y_var, b)
                    normalise(lambda t: ys[:, t, :], norm, y_rstd, y_norm, b)
                    dve.wait_ge(y_norm, TT * b + TT)
                    dve.tensor_tensor(ys[:], norm[:], gate_mid[:, ds(b), :].to_broadcast([P, TT, C]), ALU.mult).then_inc(y_gated, 1)
                    dve.wait_ge(y_gated, b + 1)
                    dve.wait_ge(xb_set, b + 1)
                    x1 = xs[:, ds(TT * b, TT), :]
                    dve.tensor_tensor(x1, x1, ys[:], ALU.add).then_inc(x1_set, 1)
                    wait_apart(dve, x1_set, b + 1)

                    layer_stats(tile_of_x(b), r_stat, r_aggr, r_var, b)
                    normalise(tile_of_x(b), norm, r_rstd, r_norm, b)
                    dve.wait_ge(rT_ps, b + 1)
                    dve.wait_ge(h2hi_set, ONE + b + 1)
                    dve.wait_ge(lg_ps, ONE + b)
                    dve.tensor_scalar(h2[:], M[:], modc[:, 3, ds(b)], modc[:, 2, ds(b)], ALU.mult, ALU.add).then_inc(h2_set, 1)
                    dve.wait_ge(h2_set, ONE + b + 1)
                    dve.tensor_tensor(h2_lo[:, ds(T * b, T)], h2[:], h2_hi[:, ds(T * b, T)].bitcast(F32), ALU.subtract).then_inc(h2lo_set, 1)
                    dve.wait_ge(lg_ps, ONE + b + 1)
                    dve.tensor_tensor(logits[:, ds(TT * b, TT), :], O[:, 0:TT * E].rearrange("p (t e) -> p t e", e=E),
                                      gate_b_all[:].unsqueeze(1).to_broadcast([P, TT, E]), ALU.add).then_inc(lg_set, 1)

                dve.wait_ge(consts_set, 3)
                dve.wait_ge(modrow_set, 4)
                dve.wait_ge(late_in, 80)
                row_maxima(0)
                with dve.Fori(0, B - 1) as b:
                    row_maxima(b + 1)
                    finish(b)
                finish(B - 1)

        with ExitStack() as ctx:
            def sb(name, shape, dt=F32):
                return ctx.enter_context(nc.sbuf_tensor(name, shape, dt))

            def ps(name, shape):
                return ctx.enter_context(nc.psum_tensor(name, shape, F32))

            HALF = N // 2
            UE = 2 * FC
            LAG = 3
            SLOTS = 4

            w1_hi = sb("w1_hi", [P, 2, F], F32R)
            w1_lo = sb("w1_lo", [P, 2, F], F32R)
            w2_hi = sb("w2_hi", [P, 2, FC, C], F32R)
            w2_lo = sb("w2_lo", [P, 2, FC, C], F32R)
            act_full = sb("act_full", [P, 2, HALF])
            act_hi = sb("act_hi", [P, SLOTS, HALF], F32R)
            act_lo = sb("act_lo", [P, SLOTS, HALF], F32R)
            gate_row = sb("gate_row", [P, 2, N])
            gated = sb("gated", [P, 2, HALF])
            acc = sb("acc", [P, N])
            order = sb("order", [P, E])
            top = sb("top", [P, 8, NT])
            pick = sb("pick", [P, 9, NT, E])
            gates = sb("gates", [P, NT, E])
            gatesT = sb("gatesT", [E, N])
            stats = sb("o_stats", [P, TT, 6])
            mv = sb("o_mv", [P, TT, 2])
            vare = sb("o_vare", [P, TT])
            rstd = sb("o_rstd", [P, TT])
            outs = sb("outs", [P, 2, TT, C])
            H1 = ps("H1", [P, 2, HALF])
            Y = ps("Y", [P, 2, HALF])

            order_set, step, masked_exp, gates_set = map(sem, ("order_set", "step", "masked_exp", "gates_set"))
            gT_ps, gT_set, bias_ps, acc_init, gates_saved = map(sem, ("gT_ps", "gT_set", "bias_ps", "acc_init", "gates_saved"))
            row_in = [sem(f"row_in{s}") for s in range(2)]
            w_hi, w_lo = sem("w_hi"), sem("w_lo")
            h_ps, gelu_full, gelu_hi, lo_set = map(sem, ("h_ps", "gelu_full", "gelu_hi", "lo_set"))
            mm2, y_done, gate_done, acc_done = map(sem, ("mm2", "y_done", "gate_done", "acc_done"))
            xo_set, outT_ps, f_stat, f_aggr, f_var, f_rstd, f_norm, f_gated, f_out, stored = map(
                sem, ("xo_set", "outT_ps", "f_stat", "f_aggr", "f_var", "f_rstd", "f_norm", "f_gated", "f_out", "stored"))

            block = ctx.enter_context(nc.Block())

            @block.sync
            def _(sp):
                sp.wait_ge(gT_set, 4)
                sp.dma_start(gates_dram[:], gatesT[:]).then_inc(gates_saved, 16)
                sp.wait_ge(gates_saved, 16)

                def load_row(e, slot):
                    sp.dma_start(gate_row[:, slot, :], gates_dram[ds(e)].to_broadcast([P, N])).then_inc(row_in[slot], 16)

                for slot in range(2):
                    load_row(slot, slot)

                with sp.Fori(0, E // 2 - 1) as i:
                    sp.wait_ge(w_lo, 4 * i + 4)
                    sp.dma_start(w1_raw[:], w1_v[:, ds(2 * i + 2, 2), :]).then_inc(w_in, 16)
                    sp.dma_start(w2_raw[:], w2_v[:, ds(2 * i + 2, 2), :, :]).then_inc(w_in, 16)
                    for slot in range(2):
                        sp.wait_ge(gate_done, 4 * i + 2 * slot + 2)
                        load_row(2 * i + 2 + slot, slot)

                for b in range(B):
                    sp.wait_ge(f_out, b + 1)
                    sp.dma_start(out_v[:, b * TT:(b + 1) * TT, :], outs[:, b % 2]).then_inc(stored, 16)
                    sp.wait_ge(stored, 16 * (b + 1))

            @block.gpsimd
            def _(pool):
                for e in range(E):
                    pool.memset(order[:, e:e + 1], float(E - e)).then_inc(order_set, 1)
                for b in range(B):
                    v = xs[:, b * TT:(b + 1) * TT, :]
                    pool.tensor_tensor(v, v, bias_out[:, b:b + 1, :].to_broadcast([P, TT, C]), ALU.add).then_inc(xo_set, 1)
                pool.wait_ge(acc_init, 4)

                def add(e, half):
                    pool.wait_ge(gate_done, 2 * e + half + 1)
                    if not (isinstance(e, int) and e == 0):
                        pool.wait_ge(acc_done, 2 * e + half - 1)
                    a = acc[:, half * HALF:(half + 1) * HALF]
                    pool.tensor_tensor(a, a, gated[:, half, :], ALU.add).then_inc(acc_done, 1)

                add(0, 0)
                add(0, 1)
                with pool.Fori(1, E) as e:
                    add(e, 0)
                    add(e, 1)
                for b in range(B):
                    pool.wait_ge(f_var, b + 1)
                    pool.tensor_tensor(rstd[:], vare[:], half_neg[:, 0:TT], ALU.pow).then_inc(f_rstd, 1)

            @block.tensor
            def _(pe):
                def first(i, u):
                    e, half, k = u // UE, u // FC % 2, u % FC
                    if u % UE == 0:
                        pe.wait_ge(w_lo, 4 * i + 2 * e + 2)
                    if isinstance(i, int) and i == 0:
                        if u >= 2:
                            pe.wait_ge(gelu_hi, u - 1)
                    else:
                        pe.wait_ge(gelu_hi, 2 * UE * i + u - 1)
                    for tb in range(2):
                        cols_ = slice(half * HALF + tb * 512, half * HALF + (tb + 1) * 512)
                        for n, (w, h) in enumerate(((w1_hi, h2_hi), (w1_hi, h2_lo), (w1_lo, h2_hi))):
                            mm = pe.matmul(H1[:, u % 2, tb * 512:(tb + 1) * 512], w[:, e, k * P:(k + 1) * P], h[:, cols_],
                                           start=(n == 0), stop=(n == 2))
                    mm.then_inc(h_ps, 1)

                def second(i, u):
                    e, half, k = u // UE, u // FC % 2, u % FC
                    pe.wait_ge(lo_set, 2 * UE * i + u + 1)
                    if k == 0:
                        done = 2 * e + half - 1
                        if not (isinstance(i, int) and 4 * i + done <= 0):
                            pe.wait_ge(gate_done, 4 * i + done)
                    for tb in range(2):
                        for n, (w, h) in enumerate(((w2_hi, act_hi), (w2_hi, act_lo), (w2_lo, act_hi))):
                            mm = pe.matmul(Y[:, half, tb * 512:(tb + 1) * 512], w[:, e, k, :],
                                           h[:, u % SLOTS, tb * 512:(tb + 1) * 512],
                                           start=(k == 0 and n == 0), stop=(k == FC - 1 and n == 2), skip_group_check=True)
                    mm.then_inc(mm2, 1)

                for u in range(LAG):
                    first(0, u)
                pe.wait_ge(gates_set, 1)
                for t in range(NT):
                    mm = pe.transpose(Y[0:E, t // 8, (t % 8) * P:(t % 8 + 1) * P], gates[:, t, :], ident[:])
                    if t % 4 == 3:
                        mm.then_inc(gT_ps, 1)
                for n in range(4):
                    pe.wait_ge(gT_set, n + 1)
                    pe.matmul(Y[:, n // 2, (n % 2) * 512:(n % 2 + 1) * 512], b2_rows[:], gatesT[:, n * 512:(n + 1) * 512],
                              start=True, stop=True).then_inc(bias_ps, 1)
                pe.wait_ge(acc_init, 4)
                for u in range(2 * UE):
                    second(0, u)
                    first(u // (2 * UE) if u + LAG < 2 * UE else 1, (u + LAG) % (2 * UE))
                with pe.Fori(1, E // 2 - 1) as i:
                    for u in range(2 * UE):
                        second(i, u)
                        first(i if u + LAG < 2 * UE else i + 1, (u + LAG) % (2 * UE))
                last = E // 2 - 1
                for u in range(2 * UE):
                    second(last, u)
                    if u + LAG < 2 * UE:
                        first(last, u + LAG)

                for b in range(B):
                    pe.wait_ge(acc_done, 2 * E - 1 + b // 2)
                    if b == 0:
                        pe.wait_ge(gate_done, 2 * E)
                    for t in range(TT):
                        mm = pe.transpose(Y[:, b // 2, (b % 2) * 512 + t * P:(b % 2) * 512 + (t + 1) * P],
                                          acc[:, (b * TT + t) * P:(b * TT + t + 1) * P], ident[:])
                    mm.then_inc(outT_ps, 1)

            @block.scalar
            def _(act):
                act.wait_ge(masked_exp, 1)
                act.activation(pick[:, 7], pick[:, 6], ACT.Exp).then_inc(masked_exp, 1)

                def gelu(i, u):
                    e, half, k = u // UE, u // FC % 2, u % FC
                    n = 2 * UE * i + u
                    bias = cols[:, ds(2 * FC * i + FC * e + k)]
                    wait_apart(act, h_ps, n + 1)
                    if not (isinstance(i, int) and n < 2):
                        wait_apart(act, lo_set, n - 1)
                    act.activation(act_full[:, u % 2, :], H1[:, u % 2, :], ACT.Gelu, bias=bias).then_inc(gelu_full, 1)
                    if not (isinstance(i, int) and n < SLOTS):
                        wait_apart(act, mm2, n - SLOTS + 1)
                    act.activation(act_hi[:, u % SLOTS, :], H1[:, u % 2, :], ACT.Gelu, bias=bias).then_inc(gelu_hi, 1)

                for u in range(2 * UE):
                    gelu(0, u)
                with act.Fori(1, E // 2) as i:
                    for u in range(2 * UE):
                        gelu(i, u)

            @block.vector
            def _(dve):
                def split(i, e):
                    if e == 0:
                        dve.wait_ge(w_in, 32 * (i + 1))
                    if not (isinstance(i, int) and i == 0):
                        dve.wait_ge(mm2, 2 * UE * (i - 1) + UE * (e + 1))
                    dve.tensor_copy(w1_hi[:, e, :], w1_raw[:, e, :]).then_inc(w_hi, 1)
                    dve.tensor_copy(w2_hi[:, e], w2_raw[:, e]).then_inc(w_hi, 1)
                    dve.wait_ge(w_hi, 4 * i + 2 * e + 1)
                    dve.tensor_tensor(w1_lo[:, e, :], w1_raw[:, e, :], w1_hi[:, e, :].bitcast(F32), ALU.subtract).then_inc(w_lo, 1)
                    dve.wait_ge(w_hi, 4 * i + 2 * e + 2)
                    dve.tensor_tensor(w2_lo[:, e], w2_raw[:, e], w2_hi[:, e].bitcast(F32), ALU.subtract).then_inc(w_lo, 1)

                split(0, 0)

                count = 0

                def then(ins):
                    nonlocal count
                    count += 1
                    ins.then_inc(step, 1)
                    dve.wait_ge(step, count)

                def wide(v):
                    return v.unsqueeze(2).to_broadcast([P, NT, E])

                lg, sel1, rest, sel2, tmp, keep, shifted, expd, kept = (pick[:, n] for n in range(9))
                then(dve.tensor_scalar(lg, logits[:], 1.0 / TEMP, None, ALU.mult))

                def largest(src, n, sel):
                    then(dve.tensor_reduce(top[:, n], src, AX.X, ALU.max))
                    then(dve.tensor_tensor(tmp, src, wide(top[:, n]), ALU.is_ge))
                    then(dve.tensor_tensor(tmp, tmp, order[:].unsqueeze(1).to_broadcast([P, NT, E]), ALU.mult))
                    then(dve.tensor_reduce(top[:, n + 1], tmp, AX.X, ALU.max))
                    then(dve.tensor_tensor(sel, tmp, wide(top[:, n + 1]), ALU.is_ge))

                dve.wait_ge(order_set, E)
                largest(lg, 0, sel1)
                dve.tensor_tensor(shifted, lg, wide(top[:, 0]), ALU.subtract).then_inc(masked_exp, 1)
                then(dve.scalar_tensor_tensor(out=rest, in0=sel1, scalar=LOWEST, in1=lg, op0=ALU.mult, op1=ALU.add))
                largest(rest, 2, sel2)
                then(dve.tensor_tensor(keep, sel1, sel2, ALU.add))
                dve.wait_ge(masked_exp, 2)
                then(dve.tensor_tensor(kept, expd, keep, ALU.mult))
                then(dve.tensor_reduce(top[:, 4], kept, AX.X, ALU.add))
                then(dve.reciprocal(top[:, 5], top[:, 4]))
                dve.tensor_tensor(gates[:], kept, wide(top[:, 5]), ALU.mult).then_inc(gates_set, 1)
                for n in range(4):
                    dve.wait_ge(gT_ps, n + 1)
                    if n < 3:
                        pass
                for n in range(4):
                    dve.tensor_copy(gatesT[:, n * 512:(n + 1) * 512], Y[0:E, n // 2, (n % 2) * 512:(n % 2 + 1) * 512]).then_inc(gT_set, 1)
                for n in range(4):
                    dve.wait_ge(bias_ps, n + 1)
                    dve.tensor_copy(acc[:, n * 512:(n + 1) * 512], Y[:, n // 2, (n % 2) * 512:(n % 2 + 1) * 512]).then_inc(acc_init, 1)

                def low(i, u):
                    n = 2 * UE * i + u
                    dve.wait_ge(gelu_hi, n + 1)
                    dve.wait_ge(gelu_full, n + 1)
                    if not (isinstance(i, int) and n < SLOTS):
                        dve.wait_ge(mm2, n - SLOTS + 1)
                    dve.tensor_tensor(act_lo[:, u % SLOTS, :], act_full[:, u % 2, :], act_hi[:, u % SLOTS, :].bitcast(F32),
                                      ALU.subtract).then_inc(lo_set, 1)

                def gate(i, g):
                    e, half = g // 2, g % 2
                    dve.wait_ge(mm2, 2 * UE * i + FC * (g + 1))
                    if half == 0:
                        dve.wait_ge(row_in[e], 16 * (i + 1))
                    if not (isinstance(i, int) and i == 0 and e == 0):
                        dve.wait_ge(acc_done, 4 * i + g - 1)
                    dve.tensor_tensor(gated[:, half, :], Y[:, half, :], gate_row[:, e, half * HALF:(half + 1) * HALF],
                                      ALU.mult).then_inc(gate_done, 1)

                def pair(i, first_pair=False, last_pair=False):
                    for u in range(2 * UE):
                        if u == UE // 2 and first_pair:
                            split(i, 1)
                        if u == UE // 2 + 1 and not first_pair:
                            split(i, 1)
                        if u == 2 * UE - 2 and not last_pair:
                            split(i + 1, 0)
                        low(i, u)
                        if u >= LAG + FC and (u - LAG) % FC == 0:
                            gate(i, (u - LAG) // FC - 1)
                        if u == LAG and not first_pair:
                            gate(i - 1, 3)

                pair(0, first_pair=True)
                with dve.Fori(1, E // 2 - 1) as i:
                    pair(i)
                pair(E // 2 - 1, last_pair=True)
                gate(E // 2 - 1, 3)

                for b in range(B):
                    dve.wait_ge(outT_ps, b + 1)
                    y = Y[:, b // 2, (b % 2) * 512:(b % 2 + 1) * 512].rearrange("p (t c) -> p t c", c=C)
                    for t in range(TT):
                        dve.bn_stats(stats[:, t, :], y[:, t, :]).then_inc(f_stat, 1)
                    for t in range(TT):
                        dve.wait_ge(f_stat, TT * b + t + 1)
                        dve.bn_aggr(mv[:, t, :], stats[:, t, :]).then_inc(f_aggr, 1)
                    dve.wait_ge(f_aggr, TT * b + TT)
                    dve.tensor_scalar(vare[:], mv[:, :, 1], EPS, None, ALU.add).then_inc(f_var, 1)
                    dve.wait_ge(f_rstd, b + 1)
                    o = outs[:, b % 2]
                    if b >= 2:
                        dve.wait_ge(stored, 16 * (b - 1))
                    for t in range(TT):
                        dve.tensor_scalar(o[:, t, :], y[:, t, :], mv[:, t, 0:1], rstd[:, t:t + 1],
                                          ALU.subtract, ALU.mult).then_inc(f_norm, 1)
                    dve.wait_ge(f_norm, TT * b + TT)
                    dve.tensor_tensor(o, o, gate_out[:, b:b + 1, :].to_broadcast([P, TT, C]), ALU.mult).then_inc(f_gated, 1)
                    dve.wait_ge(f_gated, b + 1)
                    dve.wait_ge(xo_set, b + 1)
                    dve.tensor_tensor(o, o, xs[:, b * TT:(b + 1) * TT, :], ALU.add).then_inc(f_out, 1)


_INS = ["L0_attn_x", "L0_attn_Wq", "L0_attn_bq", "L0_attn_Wk", "L0_attn_bk", "L0_attn_Wv", "L0_attn_bv",
        "L0_attn_Wo", "L0_attn_bo", "L0_attn_gamma", "L0_attn_beta", "L0_ffn_gate_w", "L0_ffn_gate_b",
        "L0_ffn_w1", "L0_ffn_b1", "L0_ffn_w2", "L0_ffn_b2", "L0_ffn_ln_g", "L0_ffn_ln_b", "L0_c", "L0_wmod"]


def kernel(**inputs):
    import numpy as np
    import concourse.bacc as bacc
    from concourse.bass_utils import run_bass_kernel_spmd

    nc = bacc.Bacc("TRN2", target_bir_lowering=False, num_devices=1)
    arrays, args = {}, []
    for name in _INS:
        a = np.ascontiguousarray(inputs[name])
        arrays[f"in_{name}"] = a
        args.append(nc.dram_tensor(f"in_{name}", a.shape, mybir.dt.from_np(a.dtype), kind="ExternalInput").ap())
    shape = inputs["L0_attn_x"].shape
    args.append(nc.dram_tensor("out_x", shape, F32, kind="ExternalOutput").ap())
    build(nc, *args)
    r = run_bass_kernel_spmd(nc, [arrays], core_ids=[0])
    return r.results[0]["out_x"]
```

```python
from contextlib import ExitStack

import concourse.bass as bass
from concourse import mybir

F32 = mybir.dt.float32
F32R = mybir.dt.float32r
ALU = mybir.AluOpType
ACT = mybir.ActivationFunctionType
AX = mybir.AxisListType

P = 128
EPS = 1e-5
TEMP = 0.9
LOWEST = -3.0e38


def ds(i, n=1):
    return bass.ds(i, n)


def build(nc, x, wq, bq, wk, bk, wv, bv, wo, bo, gamma, beta, gate_w, gate_b, w1, b1, w2, b2,
          ln_g, ln_b, c, wmod, out):
    B, T, C = x.shape
    H, DH = 16, C // 16
    E, _, F = w1.shape
    TT = T // P
    NT = B * TT
    QUADS = H // 4
    FC = F // P
    N = B * T
    assert C == P and T == 512 and DH == 8 and FC == 4
    SCALE = float(DH) ** -0.5

    ROW_BQ, ROW_BK, ROW_C, NROWS = E * FC, E * FC + 1, E * FC + 2, E * FC + 2 + B

    Q_PIECE, K_PIECE = (0, 0, 1), (0, 1, 0)
    MAX_ROW = 3 * DH
    Q_ROWS = MAX_ROW + 2
    K_ROWS = P // 4
    ONE = 1

    FILLS = [[(0, 3, 0)], [(1, 3, 0)], [(0, 2, 0), (0, 0, 384)], [(1, 2, 0), (1, 0, 384)],
             [(2, 3, 0)], [(3, 3, 0)], [(2, 2, 0), (2, 0, 384)], [(3, 2, 0), (3, 0, 384)],
             [(0, 1, 0), (2, 1, 256)], [(1, 1, 0), (3, 1, 256)]]
    NFILL = len(FILLS)
    AFTER = []
    for f in range(NFILL):
        AFTER.append((AFTER[-1] if AFTER else 0) + len(FILLS[f]))
    NMAX = AFTER[-1]
    DURING = [((QUADS - 1) * NFILL * (n + 1) + QUADS * NFILL - 1) // (QUADS * NFILL) for n in range(QUADS * NFILL)]
    UNITS = [[(0, 0, 0), (1, 0, 512)], [(2, 0, 0), (3, 0, 512)],
             [(0, 3, 0), (0, 1, 128), (1, 3, 512), (1, 1, 640)],
             [(2, 3, 0), (2, 1, 128), (3, 3, 512), (3, 1, 640)],
             [(0, 2, 0), (2, 2, 256), (1, 2, 512), (3, 2, 768)]]
    NU = len(UNITS)
    PLACE = {(h, ch): u * 1024 + col for u, parts in enumerate(UNITS) for h, ch, col in parts}
    PV_ORDER = [(0, 1), (1, 3), (3, 3), (2, 4)]

    q_rows = nc.dram_tensor("q_rows", [B, H, Q_ROWS, T], F32)
    k_rows = nc.dram_tensor("k_rows", [B, H, K_ROWS, T], F32)
    gates_dram = nc.dram_tensor("gates_dram", [E, N], F32)

    x_v = x.rearrange("b (t p) c -> p (b t) c", p=P)
    out_v = out.rearrange("b (t p) c -> p (b t) c", p=P)
    w1_v = w1.rearrange("e d f -> d e f")
    w2_v = w2.rearrange("e (k f) d -> f e k d", f=P)

    def row(v):
        return v.rearrange("(o n) -> o n", o=1).to_broadcast([P, v.shape[0]])

    with ExitStack() as whole:
        def sem(name):
            return whole.enter_context(nc.semaphore(name))

        def shared(name, shape, dt=F32):
            return whole.enter_context(nc.sbuf_tensor(name, shape, dt))

        xs = shared("xs", [P, NT, C])
        ident = shared("ident", [P, P])
        cols = shared("cols", [P, NROWS])
        half_neg = shared("half_neg", [P, NT])
        gate_out = shared("gate_out", [P, B, C])
        bias_out = shared("bias_out", [P, B, C])
        h2_hi = shared("h2_hi", [P, N], F32R)
        h2_lo = shared("h2_lo", [P, N], F32R)
        logits = shared("logits", [P, NT, E])
        gate_b_all = shared("gate_b_all", [P, E])
        w1_raw = shared("w1_raw", [P, 2, F])
        w2_raw = shared("w2_raw", [P, 2, FC, C])
        b2_rows = shared("b2_rows", [E, C])

        w_in = sem("w_in")
        go = sem("go")

        def wait_apart(eng, sem_, value):
            if not isinstance(value, int):
                value = eng.to_reg(value)
                eng.wait_ge(go, 1)
            eng.wait_ge(sem_, value)

        with ExitStack() as ctx:
            def sb(name, shape, dt=F32):
                return ctx.enter_context(nc.sbuf_tensor(name, shape, dt))

            def ps(name, shape):
                return ctx.enter_context(nc.psum_tensor(name, shape, F32))

            mask = sb("mask", [P, T])
            rows = sb("rows", [NROWS, P])
            wqs, wks, wvs, wos = (sb(n, [P, C]) for n in ("wqs", "wks", "wvs", "wos"))
            gws = sb("gws", [P, E])
            wmods = sb("wmods", [P, 6 * C])
            bv_all, bo_all, gam_all, bet_all, lng_all, lnb_all = (
                sb(n, [P, C]) for n in ("bv_all", "bo_all", "gam_all", "bet_all", "lng_all", "lnb_all"))
            sil = sb("sil", [P, 3, B])
            silu = sb("silu", [P, B])
            silu_wide = sb("silu_wide", [P, B, P])
            modc = sb("modc", [P, 4, B])
            gate_mid = sb("gate_mid", [P, B, C])
            bias_mid = sb("bias_mid", [P, B, C])
            stats = sb("stats", [P, TT, 6])
            mv = sb("mv", [P, TT, 2])
            vare = sb("vare", [P, TT])
            rstd = sb("rstd", [P, TT])
            norm = sb("norm", [P, TT, C])
            hT = sb("hT", [P, T])
            q_out = sb("q_out", [P, 2, T], F32R)
            k_out = sb("k_out", [P, 2, T], F32R)
            v_all = sb("v_all", [P, B, TT, C])
            v_pad = sb("v_pad", [P, TT, H, 32])
            qa = sb("qa", [P, 2, 4, T], F32R)
            ka = sb("ka", [P, 2, T], F32R)
            qb = sb("qb", [P, QUADS, 4, T], F32R)
            kb = sb("kb", [P, QUADS, T], F32R)
            junk = sb("junk", [P, 2, T])
            maxes = sb("maxes", [P, H * TT])
            max_out = sb("max_out", [4 * TT, QUADS, 2, P], F32R)
            probs = sb("probs", [P, 2, NU * 1024])
            clamp = probs[:, 0, 0:8 * B * C].rearrange("p (n b c) -> p n b c", b=B, c=C)
            o_spread = sb("o_spread", [P, QUADS, T])
            k_tail = probs[0:B * H, 1, 0:(K_ROWS - MAX_ROW) * T]
            rec = sb("rec", [P, TT, H])
            o_norm = sb("o_norm", [P, TT, C])
            oT = sb("oT", [P, T])
            ys = sb("ys", [P, TT, C])
            h2 = sb("h2", [P, T])

            S = ps("S", [P, 2, 1024])
            X = ps("X", [P, 2, 512])
            O = ps("O", [P, 512])
            M = ps("M", [P, 512])

            KV = S[:, 1, :].rearrange("p (n c) -> p n c", n=2)
            FIRST_BANKS = 4

            def fill_bank(b, q, f):
                n = (NFILL * q + f) % FIRST_BANKS
                if isinstance(b, int) and b == 0 and n >= 2:
                    return S[:, 0, (n - 2) * 512:(n - 1) * 512]
                return X[:, f % 2, :]

            rows_in, mod_in, proj_in, bcast_in, late_in = map(sem, ("rows_in", "mod_in", "proj_in", "bcast_in", "late_in"))
            x_in, tail_saved = sem("x_in"), sem("tail_saved")
            ident_set, consts_set, mask_set = map(sem, ("ident_set", "consts_set", "mask_set"))
            tail_set, qa_zero, qb_zero = map(sem, ("tail_set", "qa_zero", "qb_zero"))
            cols_ps, cols_set = sem("cols_ps"), sem("cols_set")
            sil_exp, sil_step = sem("sil_exp"), sem("sil_step")
            mod_ps, gmid_ps, gout_ps, modc_set, clamped, modrow_set = map(sem, ("mod_ps", "gmid_ps", "gout_ps", "modc_set", "clamped", "modrow_set"))
            x_stat, x_aggr, x_var, x_rstd, x_norm = map(sem, ("x_stat", "x_aggr", "x_var", "x_rstd", "x_norm"))
            xT_ps, hT_set, q_ps, k_ps, v_ps = map(sem, ("xT_ps", "hT_set", "q_ps", "k_ps", "v_ps"))
            q_hi, q_lo, k_hi, k_lo, v_set, qk_saved = map(sem, ("q_hi", "q_lo", "k_hi", "k_lo", "v_set", "qk_saved"))
            a_in = [sem(f"a_in{s}") for s in range(2)]
            b_in = [sem(f"b_in{q}") for q in range(QUADS)]
            fill_ps, rowmax, maxT_ps, max_hi, max_lo, max_saved = map(sem, ("fill_ps", "rowmax", "maxT_ps", "max_hi", "max_lo", "max_saved"))
            vpad_set, unit_ps, exps, masked, pv_ps, o_out = map(sem, ("vpad_set", "unit_ps", "exps", "masked", "pv_ps", "o_out"))
            oT1_ps, rec_set, onorm_set, oT2_ps, oT_set, y_ps, y_set = map(sem, ("oT1_ps", "rec_set", "onorm_set", "oT2_ps", "oT_set", "y_ps", "y_set"))
            y_stat, y_aggr, y_var, y_rstd, y_norm, y_gated, xb_set, x1_set = map(sem, ("y_stat", "y_aggr", "y_var", "y_rstd", "y_norm", "y_gated", "xb_set", "x1_set"))
            r_stat, r_aggr, r_var, r_rstd, r_norm, rT_ps = map(sem, ("r_stat", "r_aggr", "r_var", "r_rstd", "r_norm", "rT_ps"))
            h2hi_set, h2_set, h2lo_set, lg_ps, lg_set = map(sem, ("h2hi_set", "h2_set", "h2lo_set", "lg_ps", "lg_set"))

            from_one = (x_in, hT_set, q_lo, k_lo, v_set, v_ps, qk_saved, x_norm, xT_ps,
                        exps, h2hi_set, h2_set, lg_set, o_out, oT1_ps, pv_ps, y_ps, oT2_ps, lg_ps, max_saved)

            block = ctx.enter_context(nc.Block())

            @block.sync
            def _(sp):
                sp.wait_ge(go, 1)
                def load_x(b):
                    if b > 0:
                        sp.wait_ge(x_in, ONE + 16 * b)
                    sp.dma_start(xs[:, TT * b:TT * (b + 1), :], x_v[:, TT * b:TT * (b + 1), :]).then_inc(x_in, 16)

                sp.dma_start(rows[0:E * FC, :], b1.rearrange("e (k f) -> (e k) f", f=P)).then_inc(rows_in, 16)
                sp.dma_start(rows[ROW_BQ:ROW_BQ + 1, :], bq.rearrange("(o n) -> o n", o=1)).then_inc(rows_in, 16)
                sp.dma_start(rows[ROW_BK:ROW_BK + 1, :], bk.rearrange("(o n) -> o n", o=1)).then_inc(rows_in, 16)
                sp.dma_start(rows[ROW_C:NROWS, :], c).then_inc(rows_in, 16)
                load_x(0)
                sp.dma_start(wmods[:], wmod).then_inc(mod_in, 16)
                for dst, src in ((wqs, wq), (wks, wk), (wvs, wv)):
                    sp.dma_start(dst[:], src).then_inc(proj_in, 16)
                load_x(1)
                for dst, src in ((bv_all, bv), (gam_all, gamma), (bet_all, beta), (lng_all, ln_g), (lnb_all, ln_b)):
                    sp.dma_start(dst[:], row(src)).then_inc(bcast_in, 16)
                sp.wait_ge(tail_set, 2)
                sp.dma_start(k_rows[:, :, MAX_ROW:K_ROWS, :].rearrange("b h r t -> (b h) (r t)"), k_tail).then_inc(tail_saved, 16)
                load_x(2)

                def save(b):
                    for done, src, dst, piece in ((q_lo, q_out, q_rows, Q_PIECE), (k_lo, k_out, k_rows, K_PIECE)):
                        sp.wait_ge(done, ONE + b + 1)
                        for r, half in enumerate(piece):
                            sp.dma_start(dst[b, :, DH * r:DH * (r + 1), :], src[:, half, :].bitcast(F32)).then_inc(qk_saved, 16)

                def quad_of(src, b, q):
                    return src[ds(b), 4 * q:4 * q + 4].rearrange("o h r t -> (o h) r t")

                def load_a(b, q):
                    if not (isinstance(b, int) and b == 0 and q < 2):
                        wait_apart(sp, fill_ps, NFILL * (QUADS * b + q - 1))
                    sp.dma_start(ka[:, q % 2, :].bitcast(F32), quad_of(k_rows, b, q).rearrange("h r t -> (h r) t")).then_inc(a_in[q % 2], 16)
                    for j in range(4):
                        sp.dma_start(qa[K_ROWS * j:K_ROWS * j + MAX_ROW, q % 2, j, :].bitcast(F32),
                                     quad_of(q_rows, b, q)[j, 0:MAX_ROW, :]).then_inc(a_in[q % 2], 16)

                def load_b(b, nxt, q):
                    if not (isinstance(b, int) and b == 0):
                        wait_apart(sp, unit_ps, NU * (QUADS * (b - 1) + q + 1))
                    sp.dma_start(kb[:, q, :].bitcast(F32), quad_of(k_rows, b, q).rearrange("h r t -> (h r) t")).then_inc(b_in[q], 16)
                    if q + 2 < QUADS:
                        load_a(b, q + 2)
                    elif nxt is not None:
                        load_a(nxt, q + 2 - QUADS)
                    if isinstance(b, int) and b == 0 and q + 2 < B:
                        save(q + 2)
                    wait_apart(sp, max_lo, QUADS * b + q + 1)
                    for half in range(2):
                        sp.dma_start(q_rows[ds(b), 4 * q:4 * q + 4, MAX_ROW + half].rearrange("o h (t p) -> (o h) t p", p=P),
                                     max_out[:, q, half, :].bitcast(F32)).then_inc(max_saved, 16)
                    wait_apart(sp, max_saved, ONE + 32 * (QUADS * b + q + 1))
                    for j in range(4):
                        sp.dma_start(qb[K_ROWS * j:K_ROWS * j + Q_ROWS, q, j, :].bitcast(F32),
                                     quad_of(q_rows, b, q)[j]).then_inc(b_in[q], 16)

                save(0)
                load_x(3)
                sp.wait_ge(tail_saved, 16)
                sp.wait_ge(qk_saved, ONE + 96)
                sp.wait_ge(qa_zero, 1)
                load_a(0, 0)
                load_a(0, 1)
                save(1)
                for dst, src in ((bo_all, row(bo)), (gate_b_all, row(gate_b)), (wos, wo), (gws, gate_w), (b2_rows, b2)):
                    sp.dma_start(dst[:], src).then_inc(late_in, 16)
                sp.wait_ge(qb_zero, 1)
                for q in range(QUADS):
                    if q == QUADS - 2:
                        sp.wait_ge(qk_saved, ONE + 96 * B)
                    load_b(0, 1, q)
                sp.dma_start(w1_raw[:], w1_v[:, 0:2, :]).then_inc(w_in, 16)
                sp.dma_start(w2_raw[:], w2_v[:, 0:2, :, :]).then_inc(w_in, 16)
                with sp.Fori(1, B - 1) as b:
                    for q in range(QUADS):
                        load_b(b, b + 1, q)
                for q in range(QUADS):
                    load_b(B - 1, None, q)

            @block.gpsimd
            def _(pool):
                pool.memset(ident[:], 0.0).then_inc(ident_set, 1)
                for s_ in from_one:
                    pool.sem_inc(s_, ONE)
                pool.sem_inc(go, 1)
                pool.wait_ge(ident_set, 1)
                pool.affine_select(out=ident[:], in_=ident[:], compare_op=ALU.not_equal, fill=1.0, base=0,
                                   pattern=[[-1, P]], channel_multiplier=1).then_inc(ident_set, 1)
                pool.memset(half_neg[:], -0.5).then_inc(consts_set, 1)
                pool.memset(mask[:], 0.0).then_inc(mask_set, 1)
                pool.wait_ge(mask_set, 1)
                pool.affine_select(out=mask[:, T - P:T], in_=mask[:, T - P:T], compare_op=ALU.is_ge, fill=LOWEST, base=0,
                                   pattern=[[-1, P]], channel_multiplier=1).then_inc(mask_set, 1)
                pool.wait_ge(consts_set, 1)

                def inv_sqrt(var, done, b):
                    pool.wait_ge(var, b + 1)
                    pool.tensor_tensor(rstd[:], vare[:], half_neg[:, 0:TT], ALU.pow).then_inc(done, 1)

                inv_sqrt(x_var, x_rstd, 0)
                pool.memset(qb[:].bitcast(F32), 0.0).then_inc(qb_zero, 1)
                with pool.Fori(1, B) as b:
                    inv_sqrt(x_var, x_rstd, b)
                pool.memset(v_pad[:], 0.0).then_inc(consts_set, 1)
                pool.wait_ge(consts_set, 2)
                pool.memset(v_pad[:, :, :, DH:DH + 1], 1.0).then_inc(consts_set, 1)

                def attend(b):
                    for q in range(QUADS):
                        for u in range(NU):
                            wait_apart(pool, exps, ONE + NU * (QUADS * b + q) + u + 1)
                            if u < 2:
                                v = probs[:, q % 2, ds(u * 1024, 1024)].rearrange("p (h c) -> p h c", h=2)[:, :, 0:P]
                                pattern = [[0, 2], [1, P]]
                            elif u < 4:
                                v = probs[:, q % 2, ds(u * 1024, 1024)].rearrange("p (h c) -> p h c", h=2)[:, :, 0:2 * P]
                                pattern = [[0, 2], [0, 2], [1, P]]
                            else:
                                v = probs[:, q % 2, ds(u * 1024, 1024)].rearrange("p (h c) -> p h c", h=4)[:, :, 0:P]
                                pattern = [[0, 4], [1, P]]
                            pool.affine_select(out=v, in_=v, compare_op=ALU.is_ge, fill=0.0, base=0,
                                               pattern=pattern, channel_multiplier=-1).then_inc(masked, 1)

                def finish(b):
                    pool.tensor_tensor(xs[:, ds(TT * b, TT), :], xs[:, ds(TT * b, TT), :],
                                       bias_mid[:, ds(b), :].to_broadcast([P, TT, C]), ALU.add).then_inc(xb_set, 1)
                    inv_sqrt(y_var, y_rstd, b)
                    inv_sqrt(r_var, r_rstd, b)

                pool.wait_ge(modrow_set, 4)
                pool.wait_ge(x_norm, ONE + NT)
                with pool.Fori(0, B - 1) as b:
                    attend(b)
                    finish(b)
                attend(B - 1)
                finish(B - 1)

            @block.tensor
            def _(pe):
                pe.wait_ge(go, 1)
                pe.wait_ge(ident_set, 2)
                pe.wait_ge(rows_in, 64)
                pe.transpose(M[:, 0:NROWS], rows[:], ident[0:NROWS, 0:NROWS]).then_inc(cols_ps, 1)
                pe.wait_ge(sil_step, 4)
                pe.wait_ge(mod_in, 16)
                for n, j in enumerate((0, 1, 3, 4)):
                    mm = pe.matmul(O[:, n * B:(n + 1) * B], wmods[:, j * C:(j + 1) * C], silu[:], start=True, stop=True)
                mm.then_inc(mod_ps, 1)
                pe.wait_ge(proj_in, 48)
                pe.wait_ge(cols_set, 1)
                pe.wait_ge(modc_set, 2)

                def turn_x(b):
                    pe.wait_ge(x_norm, ONE + TT * b + TT)
                    pe.wait_ge(hT_set, ONE + b)
                    if b >= 3:
                        pe.wait_ge(max_lo, b - 2)
                    for t in range(TT):
                        mm = pe.transpose(M[:, t * P:(t + 1) * P], norm[:, t, :], ident[:])
                    mm.then_inc(xT_ps, 1)

                def project_qk(b):
                    pe.wait_ge(hT_set, ONE + b + 1)
                    pe.wait_ge(q_lo, ONE + b)
                    pe.matmul(O[:], wqs[:], hT[:], start=True, stop=True).then_inc(q_ps, 1)
                    pe.wait_ge(k_lo, ONE + b)
                    pe.matmul(KV[:, 0, :], wks[:], hT[:], start=True, stop=True).then_inc(k_ps, 1)

                def project_v(b):
                    pe.wait_ge(v_set, ONE + b)
                    for t in range(TT):
                        mm = pe.matmul(KV[:, 1, t * C:(t + 1) * C], hT[:, t * P:(t + 1) * P], wvs[:], start=True, stop=True)
                    mm.then_inc(v_ps, 1)

                def rowmax_fill(b, q, f):
                    if f == 0:
                        pe.wait_ge(a_in[q % 2], 80 * (2 * b + q // 2 + 1))
                    if isinstance(b, int) and b == 0:
                        before = NFILL * q + f - FIRST_BANKS
                        if before >= 0:
                            pe.wait_ge(rowmax, NMAX * (before // NFILL) + AFTER[before % NFILL])
                        if NFILL * q + f == 2:
                            pe.wait_ge(clamped, 8)
                    else:
                        before = AFTER[f - 2] if f >= 2 else AFTER[f - 2] - NMAX
                        pe.wait_ge(rowmax, NMAX * (QUADS * b + q) + before)
                    for head, tile, col in FILLS[f]:
                        mm = pe.matmul(fill_bank(b, q, f)[:, col:col + P * (tile + 1)], qa[:, q % 2, head, tile * P:(tile + 1) * P],
                                       ka[:, q % 2, 0:P * (tile + 1)], start=True, stop=True, skip_group_check=True)
                    mm.then_inc(fill_ps, 1)

                def max_turn(b, q):
                    pe.wait_ge(rowmax, NMAX * (QUADS * b + q + 1))
                    pe.wait_ge(max_lo, QUADS * b + q)
                    if isinstance(b, int) and b == 0:
                        pe.wait_ge(hT_set, ONE + min(q + 3, B))
                    else:
                        ended = b if q == QUADS - 1 else b - 1
                        pe.wait_ge(h2hi_set, ONE + ended)
                        pe.wait_ge(h2_set, ONE + ended)
                    pe.transpose(M[0:4 * TT, 0:P], maxes[:, 4 * TT * q:4 * TT * (q + 1)], ident[:]).then_inc(maxT_ps, 1)

                def scores(b, q, u):
                    if u == 0:
                        pe.wait_ge(b_in[q], 80 * (b + 1))
                    pe.wait_ge(exps, ONE + NU * QUADS * b + max(NU * q + u - 1, 0))
                    slot = (NU * q + u) % 2
                    for head, ch, col in UNITS[u]:
                        mm = pe.matmul(S[:, slot, col:col + T - P * ch], kb[:, q, ch * P:(ch + 1) * P],
                                       qb[:, q, head, ch * P:T], start=True, stop=True, skip_group_check=True)
                    mm.then_inc(unit_ps, 1)

                def values(b, q, n):
                    ch, unit = PV_ORDER[n]
                    if n == 0:
                        if q == 0:
                            pe.wait_ge(vpad_set, b + 1)
                            pe.wait_ge(lg_set, ONE + b)
                        pe.wait_ge(o_out, ONE + QUADS * b + q)
                    pe.wait_ge(masked, NU * (QUADS * b + q) + unit + 1)
                    for j in range(4):
                        at = PLACE[j, ch]
                        mm = pe.matmul(O[32 * j:32 * j + 32, ch * P:T], v_pad[:, ch, 4 * q + j, :],
                                       probs[:, q % 2, at:at + T - P * ch], start=(n == 0), stop=(n == TT - 1),
                                       tile_position=(0, 32 * j), skip_group_check=True)
                    if n == TT - 1:
                        mm.then_inc(pv_ps, 1)

                def attend(b, nxt):
                    for q in range(QUADS):
                        for s in range(NFILL):
                            if s % 2 == 0:
                                scores(b, q, s // 2)
                            if nxt is not None:
                                n = DURING[NFILL * q + s]
                                for m in range(DURING[NFILL * q + s - 1] if q + s else 0, n):
                                    rowmax_fill(nxt, m // NFILL, m % NFILL)
                                    if m % NFILL == 1 and m > NFILL:
                                        max_turn(nxt, m // NFILL - 1)
                            if s % 2 == 1 and s < 9 and q >= 1:
                                values(b, q - 1, s // 2)
                    for n in range(TT):
                        values(b, QUADS - 1, n)
                    if nxt is not None:
                        max_turn(nxt, QUADS - 2)

                def finish(b, nxt):
                    def fills(*fs):
                        if nxt is not None:
                            for f in fs:
                                rowmax_fill(nxt, QUADS - 1, f)

                    fills(0, 1)
                    pe.wait_ge(o_out, ONE + QUADS * b + QUADS)
                    if nxt is not None:
                        pe.wait_ge(max_lo, QUADS * nxt + QUADS - 1)
                    for t in range(TT):
                        bank = (M, O)[t % 2]
                        if t >= 2:
                            pe.wait_ge(onorm_set, TT * b + t - 1)
                        for q in range(QUADS):
                            mm = pe.transpose(bank[:, q * P:(q + 1) * P], o_spread[:, q, t * P:(t + 1) * P], ident[:])
                        mm.then_inc(oT1_ps, 1)
                    for t in range(TT):
                        pe.wait_ge(onorm_set, TT * b + max(t, 2) + 1)
                        mm = pe.transpose(M[:, t * P:(t + 1) * P], o_norm[:, t, :], ident[:])
                    mm.then_inc(oT2_ps, 1)
                    fills(2)
                    pe.wait_ge(oT_set, b + 1)
                    for t in range(TT):
                        mm = pe.matmul(O[:, t * C:(t + 1) * C], oT[:, t * P:(t + 1) * P], wos[:], start=True, stop=True)
                    mm.then_inc(y_ps, 1)
                    fills(3, 4, 5, 6, 7, 8)
                    for t in range(TT):
                        pe.wait_ge(r_norm, TT * b + t + 1)
                        mm = pe.transpose(M[:, t * P:(t + 1) * P], norm[:, t, :], ident[:])
                    mm.then_inc(rT_ps, 1)
                    fills(9)
                    pe.wait_ge(h2_set, ONE + b + 1)
                    for t in range(TT):
                        mm = pe.matmul(O[:, t * E:(t + 1) * E], h2[:, t * P:(t + 1) * P], gws[:], start=True, stop=True)
                    mm.then_inc(lg_ps, 1)
                    if nxt is not None:
                        max_turn(nxt, QUADS - 1)

                turn_x(0)
                project_qk(0)
                project_v(0)
                turn_x(1)
                for j, bank, done in ((2, 0, gmid_ps), (5, 1, gout_ps)):
                    for b in range(B):
                        mm = pe.matmul(S[:, 0, ds(bank * 512 + b * C, C)], silu_wide[:, b, :], wmods[:, j * C:(j + 1) * C],
                                       start=True, stop=True)
                    mm.then_inc(done, 1)
                project_qk(1)
                project_v(1)
                for q in range(QUADS):
                    for f in range(NFILL):
                        rowmax_fill(0, q, f)
                        if f == 5 and q >= 1:
                            max_turn(0, q - 1)
                        if f == 8 and q + 2 < B:
                            turn_x(q + 2)
                        if f == 1 and 0 < q < B - 1:
                            project_qk(q + 1)
                        if f == 2 and 0 < q < B - 1:
                            project_v(q + 1)
                max_turn(0, QUADS - 1)
                pe.wait_ge(q_lo, ONE + B)
                pe.wait_ge(k_lo, ONE + B)
                pe.wait_ge(v_set, ONE + B)
                pe.wait_ge(rowmax, NMAX * QUADS)
                pe.wait_ge(consts_set, 3)
                pe.wait_ge(late_in, 80)
                with pe.Fori(0, B - 1) as b:
                    attend(b, b + 1)
                    finish(b, b + 1)
                attend(B - 1, None)
                finish(B - 1, None)

            @block.scalar
            def _(act):
                act.wait_ge(go, 1)
                act.wait_ge(cols_ps, 1)
                act.activation(cols[:], M[:, 0:NROWS], ACT.Copy).then_inc(cols_set, 1)
                act.wait_ge(cols_set, 1)
                act.activation(sil[:, 0, :], cols[:, ROW_C:ROW_C + B], ACT.Exp, scale=-1.0).then_inc(sil_exp, 1)

                with act.Fori(0, B) as b:
                    act.wait_ge(modc_set, 2)
                    wait_apart(act, xT_ps, ONE + b + 1)
                    wait_apart(act, v_ps, ONE + b)
                    act.activation(hT[:], M[:], ACT.Identity, scale=modc[:, 1, ds(b)], bias=modc[:, 0, ds(b)]).then_inc(hT_set, 1)
                    act.wait_ge(qk_saved, ONE + 96 * b)
                    act.wait_ge(q_ps, b + 1)
                    act.activation(q_out[:, 0, :], O[:], ACT.Identity, bias=cols[:, ROW_BQ:ROW_BQ + 1]).then_inc(q_hi, 1)
                    act.wait_ge(k_ps, b + 1)
                    act.activation(k_out[:, 0, :], KV[:, 0, :], ACT.Identity, bias=cols[:, ROW_BK:ROW_BK + 1]).then_inc(k_hi, 1)

                def o_copy(b, q):
                    act.wait_ge(pv_ps, ONE + QUADS * b + q + 1)
                    if q == 0:
                        act.wait_ge(oT1_ps, ONE + TT * b)
                    act.activation(o_spread[:, q, :], O[:], ACT.Copy).then_inc(o_out, 1)

                def attend(b):
                    wait_apart(act, pv_ps, ONE + QUADS * b)
                    act.activation(v_pad[:, :, :, 0:DH], v_all[:, ds(b), :, :].rearrange("p o t (h i) -> p (o t) h i", i=DH),
                                   ACT.Copy).then_inc(vpad_set, 1)
                    for q in range(QUADS):
                        if q >= 2:
                            act.wait_ge(pv_ps, ONE + QUADS * b + q - 1)
                        for u in range(NU):
                            act.wait_ge(unit_ps, NU * (QUADS * b + q) + u + 1)
                            act.activation(probs[:, q % 2, u * 1024:(u + 1) * 1024], S[:, (NU * q + u) % 2, :],
                                           ACT.Exp, scale=SCALE).then_inc(exps, 1)
                        if q >= 1:
                            o_copy(b, q - 1)
                    o_copy(b, QUADS - 1)

                def finish(b):
                    act.wait_ge(oT2_ps, ONE + b + 1)
                    act.wait_ge(y_ps, ONE + b)
                    act.activation(oT[:], M[:], ACT.Copy).then_inc(oT_set, 1)
                    wait_apart(act, rT_ps, b + 1)
                    act.activation(h2_hi[:, ds(T * b, T)], M[:], ACT.Identity, scale=modc[:, 3, ds(b)],
                                   bias=modc[:, 2, ds(b)]).then_inc(h2hi_set, 1)

                act.wait_ge(v_set, ONE + B)
                act.wait_ge(consts_set, 3)
                with act.Fori(0, B - 1) as b:
                    attend(b)
                    finish(b)
                attend(B - 1)
                finish(B - 1)

            @block.vector
            def _(dve):
                dve.wait_ge(go, 1)
                dve.memset(k_tail[:, 0:2 * T], 1.0).then_inc(tail_set, 1)
                dve.memset(k_tail[:, 2 * T:], 0.0).then_inc(tail_set, 1)

                def layer_stats(src, stat, aggr, var, b):
                    for t in range(TT):
                        dve.bn_stats(stats[:, t, :], src(t)).then_inc(stat, 1)
                    for t in range(TT):
                        wait_apart(dve, stat, TT * b + t + 1)
                        dve.bn_aggr(mv[:, t, :], stats[:, t, :]).then_inc(aggr, 1)
                    dve.wait_ge(aggr, TT * b + TT)
                    dve.tensor_scalar(vare[:], mv[:, :, 1], EPS, None, ALU.add).then_inc(var, 1)

                def normalise(src, dst, rs, done, b):
                    dve.wait_ge(rs, b + 1)
                    for t in range(TT):
                        dve.tensor_scalar(dst[:, t, :], src(t), mv[:, t, 0:1], rstd[:, t:t + 1],
                                          ALU.subtract, ALU.mult).then_inc(done, 1)

                def tile_of_x(b):
                    return lambda t: xs[:, ds(TT * b + t), :].rearrange("p o c -> p (o c)")

                def x_stats(b):
                    dve.wait_ge(x_in, ONE + 16 * b + 16)
                    wait_apart(dve, x_norm, ONE + TT * b)
                    layer_stats(tile_of_x(b), x_stat, x_aggr, x_var, b)

                def project_low(b):
                    dve.wait_ge(q_hi, b + 1)
                    dve.scalar_tensor_tensor(out=q_out[:, 1, :], in0=O[:], scalar=cols[:, ROW_BQ:ROW_BQ + 1],
                                             in1=q_out[:, 0, :].bitcast(F32), op0=ALU.add, op1=ALU.subtract).then_inc(q_lo, 1)
                    dve.wait_ge(k_hi, b + 1)
                    dve.scalar_tensor_tensor(out=k_out[:, 1, :], in0=KV[:, 0, :], scalar=cols[:, ROW_BK:ROW_BK + 1],
                                             in1=k_out[:, 0, :].bitcast(F32), op0=ALU.add, op1=ALU.subtract).then_inc(k_lo, 1)

                def project_value(b):
                    dve.wait_ge(v_ps, ONE + b + 1)
                    dve.wait_ge(bcast_in, 80)
                    dve.tensor_tensor(v_all[:, b, :, :], KV[:, 1, :].rearrange("p (t c) -> p t c", c=C),
                                      bv_all[:].unsqueeze(1).to_broadcast([P, TT, C]), ALU.add).then_inc(v_set, 1)

                def normalise_x(b):
                    dve.wait_ge(xT_ps, ONE + b)
                    normalise(tile_of_x(b), norm, x_rstd, x_norm, b)

                x_stats(0)
                dve.wait_ge(sil_exp, 1)
                dve.tensor_scalar(sil[:, 1, :], sil[:, 0, :], 1.0, None, ALU.add).then_inc(sil_step, 1)
                dve.wait_ge(sil_step, 1)
                dve.reciprocal(sil[:, 2, :], sil[:, 1, :]).then_inc(sil_step, 1)
                dve.wait_ge(sil_step, 2)
                dve.tensor_tensor(silu[:], cols[:, ROW_C:ROW_C + B], sil[:, 2, :], ALU.mult).then_inc(sil_step, 1)
                dve.wait_ge(sil_step, 3)
                dve.tensor_copy(silu_wide[:], silu[:].unsqueeze(2).to_broadcast([P, B, P])).then_inc(sil_step, 1)
                normalise_x(0)
                dve.wait_ge(mod_ps, 1)
                mods = O[:, 0:4 * B].rearrange("p (n b) -> p n b", b=B)
                dve.tensor_copy(modc[:, 0:4:2, :], mods[:, 0:4:2, :]).then_inc(modc_set, 1)
                dve.tensor_scalar(modc[:, 1:4:2, :], mods[:, 1:4:2, :], 1.0, None, ALU.add).then_inc(modc_set, 1)

                x_stats(1)
                project_low(0)
                normalise_x(1)
                project_value(0)
                dve.memset(qa[:].bitcast(F32), 0.0).then_inc(qa_zero, 1)
                x_stats(2)

                for n, (done, bank, wt, bs, g_dst, b_dst) in enumerate((
                        (gmid_ps, 0, gam_all, bet_all, gate_mid, bias_mid),
                        (gout_ps, 1, lng_all, lnb_all, gate_out, bias_out))):
                    g = S[:, 0, bank * 512:bank * 512 + 512].rearrange("p (b c) -> p b c", c=C)
                    dve.wait_ge(done, 1)
                    twice, sign, size, signed = (clamp[:, 4 * n + k] for k in range(4))
                    dve.tensor_scalar(twice, g, 0.0, 2.0, ALU.is_ge, ALU.mult).then_inc(clamped, 1)
                    dve.wait_ge(clamped, 4 * n + 1)
                    dve.tensor_scalar(sign, twice, -1.0, None, ALU.add).then_inc(clamped, 1)
                    dve.scalar_tensor_tensor(out=size, in0=twice, scalar=-1.0, in1=g, op0=ALU.add, op1=ALU.mult).then_inc(clamped, 1)
                    dve.wait_ge(clamped, 4 * n + 3)
                    dve.scalar_tensor_tensor(out=signed, in0=size, scalar=0.25, in1=sign, op0=ALU.max, op1=ALU.mult).then_inc(clamped, 1)
                    dve.wait_ge(clamped, 4 * n + 4)
                    dve.tensor_tensor(g_dst[:], signed, wt[:].unsqueeze(1).to_broadcast([P, B, C]), ALU.mult).then_inc(modrow_set, 1)
                    dve.tensor_tensor(b_dst[:], signed, bs[:].unsqueeze(1).to_broadcast([P, B, C]), ALU.mult).then_inc(modrow_set, 1)

                project_low(1)
                project_value(1)

                def max_fill(b, q, f):
                    wait_apart(dve, fill_ps, NFILL * (QUADS * b + q) + f + 1)
                    k = AFTER[f] - len(FILLS[f])
                    for n, (head, tile, col) in enumerate(FILLS[f]):
                        if not (isinstance(b, int) and b == 0 and q == 0 and k + n < 2):
                            wait_apart(dve, rowmax, NMAX * (QUADS * b + q) + k + n - 1)
                        width = P * (tile + 1)
                        at = TT * (4 * q + head) + tile
                        dve.tensor_tensor_reduce(out=junk[:, (k + n) % 2, 0:width], in0=fill_bank(b, q, f)[:, col:col + width],
                                                 in1=mask[:, T - width:T], scale=1.0, scalar=LOWEST, op0=ALU.add,
                                                 op1=ALU.max, accum_out=maxes[:, at:at + 1]).then_inc(rowmax, 1)

                def max_split(b, q):
                    dve.wait_ge(maxT_ps, QUADS * b + q + 1)
                    dve.wait_ge(max_saved, ONE + 32 * QUADS * b)
                    turned = M[0:4 * TT, 0:P]
                    dve.tensor_scalar(max_out[:, q, 0, :], turned, -1.0, None, ALU.mult).then_inc(max_hi, 1)
                    dve.wait_ge(max_hi, QUADS * b + q + 1)
                    dve.scalar_tensor_tensor(out=max_out[:, q, 1, :], in0=turned, scalar=-1.0, in1=max_out[:, q, 0, :].bitcast(F32),
                                             op0=ALU.mult, op1=ALU.subtract).then_inc(max_lo, 1)

                def row_maxima(b, quads):
                    for q in range(quads):
                        for f in range(NFILL):
                            max_fill(b, q, f)
                            if f == 1 and q >= 1:
                                max_split(b, q - 1)
                    max_split(b, quads - 1)

                def finish(b, nxt):
                    def fills(*fs):
                        if nxt is not None:
                            for f in fs:
                                max_fill(nxt, QUADS - 1, f)

                    fills(0)
                    for t in range(TT):
                        dve.wait_ge(oT1_ps, ONE + TT * b + t + 1)
                        o = (M, O)[t % 2][:].rearrange("p (h i) -> p h i", i=32)
                        dve.reciprocal(rec[:, t, :], o[:, :, DH]).then_inc(rec_set, 1)
                        dve.wait_ge(rec_set, TT * b + t + 1)
                        dve.wait_ge(oT2_ps, ONE + b)
                        dve.tensor_tensor(o_norm[:, t, :].rearrange("p (h i) -> p h i", i=DH), o[:, :, 0:DH],
                                          rec[:, t, :].unsqueeze(2).to_broadcast([P, H, DH]), ALU.mult).then_inc(onorm_set, 1)
                    fills(1)
                    dve.wait_ge(y_ps, ONE + b + 1)
                    dve.tensor_tensor(ys[:], O[:].rearrange("p (t c) -> p t c", c=C),
                                      bo_all[:].unsqueeze(1).to_broadcast([P, TT, C]), ALU.add).then_inc(y_set, 1)
                    wait_apart(dve, y_set, b + 1)
                    layer_stats(lambda t: ys[:, t, :], y_stat, y_aggr, y_var, b)
                    fills(2, 3)
                    normalise(lambda t: ys[:, t, :], norm, y_rstd, y_norm, b)
                    dve.wait_ge(y_norm, TT * b + TT)
                    dve.tensor_tensor(ys[:], norm[:], gate_mid[:, ds(b), :].to_broadcast([P, TT, C]), ALU.mult).then_inc(y_gated, 1)
                    dve.wait_ge(y_gated, b + 1)
                    dve.wait_ge(xb_set, b + 1)
                    x1 = xs[:, ds(TT * b, TT), :]
                    dve.tensor_tensor(x1, x1, ys[:], ALU.add).then_inc(x1_set, 1)
                    wait_apart(dve, x1_set, b + 1)

                    layer_stats(tile_of_x(b), r_stat, r_aggr, r_var, b)
                    fills(4, 5)
                    normalise(tile_of_x(b), norm, r_rstd, r_norm, b)
                    fills(6, 7, 8)
                    dve.wait_ge(rT_ps, b + 1)
                    dve.wait_ge(h2hi_set, ONE + b + 1)
                    dve.wait_ge(lg_ps, ONE + b)
                    dve.tensor_scalar(h2[:], M[:], modc[:, 3, ds(b)], modc[:, 2, ds(b)], ALU.mult, ALU.add).then_inc(h2_set, 1)
                    dve.wait_ge(h2_set, ONE + b + 1)
                    dve.tensor_tensor(h2_lo[:, ds(T * b, T)], h2[:], h2_hi[:, ds(T * b, T)].bitcast(F32), ALU.subtract).then_inc(h2lo_set, 1)
                    fills(9)
                    dve.wait_ge(lg_ps, ONE + b + 1)
                    dve.tensor_tensor(logits[:, ds(TT * b, TT), :], O[:, 0:TT * E].rearrange("p (t e) -> p t e", e=E),
                                      gate_b_all[:].unsqueeze(1).to_broadcast([P, TT, E]), ALU.add).then_inc(lg_set, 1)
                    if nxt is not None:
                        max_split(nxt, QUADS - 1)

                dve.wait_ge(mask_set, 2)
                for q in range(QUADS):
                    for f in range(NFILL):
                        max_fill(0, q, f)
                        if f == 5 and q >= 1:
                            max_split(0, q - 1)
                        if f == 4 and q + 2 < B:
                            normalise_x(q + 2)
                        if f == 6 and q + 3 < B:
                            x_stats(q + 3)
                        if f == 2 and 0 < q < B - 1:
                            project_low(q + 1)
                        if f == 3 and 0 < q < B - 1:
                            project_value(q + 1)
                max_split(0, QUADS - 1)
                dve.wait_ge(modrow_set, 4)
                dve.wait_ge(late_in, 80)
                with dve.Fori(0, B - 1) as b:
                    row_maxima(b + 1, QUADS - 1)
                    finish(b, b + 1)
                finish(B - 1, None)

        with ExitStack() as ctx:
            def sb(name, shape, dt=F32):
                return ctx.enter_context(nc.sbuf_tensor(name, shape, dt))

            def ps(name, shape):
                return ctx.enter_context(nc.psum_tensor(name, shape, F32))

            HALF = N // 2
            UE = 2 * FC
            LAG = 3
            SLOTS = 4

            w1_hi = sb("w1_hi", [P, 2, F], F32R)
            w1_lo = sb("w1_lo", [P, 2, F], F32R)
            w2_hi = sb("w2_hi", [P, 2, FC, C], F32R)
            w2_lo = sb("w2_lo", [P, 2, FC, C], F32R)
            act_full = sb("act_full", [P, 2, HALF])
            act_hi = sb("act_hi", [P, SLOTS, HALF], F32R)
            act_lo = sb("act_lo", [P, SLOTS, HALF], F32R)
            gate_row = sb("gate_row", [P, 2, N])
            gated = sb("gated", [P, 2, HALF])
            acc = sb("acc", [P, N])
            order = sb("order", [P, E])
            top = sb("top", [P, 8, NT])
            pick = sb("pick", [P, 9, NT, E])
            gates = sb("gates", [P, NT, E])
            gatesT = sb("gatesT", [E, N])
            stats = sb("o_stats", [P, TT, 6])
            mv = sb("o_mv", [P, TT, 2])
            vare = sb("o_vare", [P, TT])
            rstd = sb("o_rstd", [P, TT])
            outs = sb("outs", [P, 2, TT, C])
            H1 = ps("H1", [P, 2, HALF])
            Y = ps("Y", [P, 2, HALF])

            order_set, step, masked_exp, gates_set = map(sem, ("order_set", "step", "masked_exp", "gates_set"))
            gT_ps, gT_set, bias_ps, acc_init, gates_saved = map(sem, ("gT_ps", "gT_set", "bias_ps", "acc_init", "gates_saved"))
            row_in = [sem(f"row_in{s}") for s in range(2)]
            w_hi, w_lo = sem("w_hi"), sem("w_lo")
            h_ps, gelu_full, gelu_hi, lo_set = map(sem, ("h_ps", "gelu_full", "gelu_hi", "lo_set"))
            mm2, y_done, gate_done, acc_done = map(sem, ("mm2", "y_done", "gate_done", "acc_done"))
            xo_set, outT_ps, f_stat, f_aggr, f_var, f_rstd, f_norm, f_gated, f_out, stored = map(
                sem, ("xo_set", "outT_ps", "f_stat", "f_aggr", "f_var", "f_rstd", "f_norm", "f_gated", "f_out", "stored"))

            block = ctx.enter_context(nc.Block())

            @block.sync
            def _(sp):
                sp.wait_ge(gT_set, 4)
                sp.dma_start(gates_dram[:], gatesT[:]).then_inc(gates_saved, 16)
                sp.wait_ge(gates_saved, 16)

                def load_row(e, slot):
                    sp.dma_start(gate_row[:, slot, :], gates_dram[ds(e)].to_broadcast([P, N])).then_inc(row_in[slot], 16)

                for slot in range(2):
                    load_row(slot, slot)

                with sp.Fori(0, E // 2 - 1) as i:
                    sp.wait_ge(w_lo, 4 * i + 4)
                    sp.dma_start(w1_raw[:], w1_v[:, ds(2 * i + 2, 2), :]).then_inc(w_in, 16)
                    sp.dma_start(w2_raw[:], w2_v[:, ds(2 * i + 2, 2), :, :]).then_inc(w_in, 16)
                    for slot in range(2):
                        sp.wait_ge(gate_done, 4 * i + 2 * slot + 2)
                        load_row(2 * i + 2 + slot, slot)

                for b in range(B):
                    sp.wait_ge(f_out, b + 1)
                    sp.dma_start(out_v[:, b * TT:(b + 1) * TT, :], outs[:, b % 2]).then_inc(stored, 16)
                    sp.wait_ge(stored, 16 * (b + 1))

            @block.gpsimd
            def _(pool):
                for e in range(E):
                    pool.memset(order[:, e:e + 1], float(E - e)).then_inc(order_set, 1)
                for b in range(B):
                    v = xs[:, b * TT:(b + 1) * TT, :]
                    pool.tensor_tensor(v, v, bias_out[:, b:b + 1, :].to_broadcast([P, TT, C]), ALU.add).then_inc(xo_set, 1)
                pool.wait_ge(acc_init, 4)

                def add(e, half):
                    pool.wait_ge(gate_done, 2 * e + half + 1)
                    if not (isinstance(e, int) and e == 0):
                        pool.wait_ge(acc_done, 2 * e + half - 1)
                    a = acc[:, half * HALF:(half + 1) * HALF]
                    pool.tensor_tensor(a, a, gated[:, half, :], ALU.add).then_inc(acc_done, 1)

                add(0, 0)
                add(0, 1)
                with pool.Fori(1, E) as e:
                    add(e, 0)
                    add(e, 1)
                for b in range(B):
                    pool.wait_ge(f_var, b + 1)
                    pool.tensor_tensor(rstd[:], vare[:], half_neg[:, 0:TT], ALU.pow).then_inc(f_rstd, 1)

            @block.tensor
            def _(pe):
                def first(i, u):
                    e, half, k = u // UE, u // FC % 2, u % FC
                    if u % UE == 0:
                        pe.wait_ge(w_lo, 4 * i + 2 * e + 2)
                    if isinstance(i, int) and i == 0:
                        if u >= 2:
                            pe.wait_ge(gelu_hi, u - 1)
                    else:
                        pe.wait_ge(gelu_hi, 2 * UE * i + u - 1)
                    for tb in range(2):
                        cols_ = slice(half * HALF + tb * 512, half * HALF + (tb + 1) * 512)
                        for n, (w, h) in enumerate(((w1_hi, h2_hi), (w1_hi, h2_lo), (w1_lo, h2_hi))):
                            mm = pe.matmul(H1[:, u % 2, tb * 512:(tb + 1) * 512], w[:, e, k * P:(k + 1) * P], h[:, cols_],
                                           start=(n == 0), stop=(n == 2))
                    mm.then_inc(h_ps, 1)

                def second(i, u):
                    e, half, k = u // UE, u // FC % 2, u % FC
                    pe.wait_ge(lo_set, 2 * UE * i + u + 1)
                    if k == 0:
                        done = 2 * e + half - 1
                        if not (isinstance(i, int) and 4 * i + done <= 0):
                            pe.wait_ge(gate_done, 4 * i + done)
                    for tb in range(2):
                        for n, (w, h) in enumerate(((w2_hi, act_hi), (w2_hi, act_lo), (w2_lo, act_hi))):
                            mm = pe.matmul(Y[:, half, tb * 512:(tb + 1) * 512], w[:, e, k, :],
                                           h[:, u % SLOTS, tb * 512:(tb + 1) * 512],
                                           start=(k == 0 and n == 0), stop=(k == FC - 1 and n == 2), skip_group_check=True)
                    mm.then_inc(mm2, 1)

                for u in range(LAG):
                    first(0, u)
                pe.wait_ge(gates_set, 1)
                for t in range(NT):
                    mm = pe.transpose(Y[0:E, t // 8, (t % 8) * P:(t % 8 + 1) * P], gates[:, t, :], ident[:])
                    if t % 4 == 3:
                        mm.then_inc(gT_ps, 1)
                for n in range(4):
                    pe.wait_ge(gT_set, n + 1)
                    pe.matmul(Y[:, n // 2, (n % 2) * 512:(n % 2 + 1) * 512], b2_rows[:], gatesT[:, n * 512:(n + 1) * 512],
                              start=True, stop=True).then_inc(bias_ps, 1)
                pe.wait_ge(acc_init, 4)
                for u in range(2 * UE):
                    second(0, u)
                    first(u // (2 * UE) if u + LAG < 2 * UE else 1, (u + LAG) % (2 * UE))
                with pe.Fori(1, E // 2 - 1) as i:
                    for u in range(2 * UE):
                        second(i, u)
                        first(i if u + LAG < 2 * UE else i + 1, (u + LAG) % (2 * UE))
                last = E // 2 - 1
                for u in range(2 * UE):
                    second(last, u)
                    if u + LAG < 2 * UE:
                        first(last, u + LAG)

                for b in range(B):
                    pe.wait_ge(acc_done, 2 * E - 1 + b // 2)
                    if b == 0:
                        pe.wait_ge(gate_done, 2 * E)
                    for t in range(TT):
                        mm = pe.transpose(Y[:, b // 2, (b % 2) * 512 + t * P:(b % 2) * 512 + (t + 1) * P],
                                          acc[:, (b * TT + t) * P:(b * TT + t + 1) * P], ident[:])
                    mm.then_inc(outT_ps, 1)

            @block.scalar
            def _(act):
                act.wait_ge(masked_exp, 1)
                act.activation(pick[:, 7], pick[:, 6], ACT.Exp).then_inc(masked_exp, 1)

                def gelu(i, u):
                    e, half, k = u // UE, u // FC % 2, u % FC
                    n = 2 * UE * i + u
                    bias = cols[:, ds(2 * FC * i + FC * e + k)]
                    wait_apart(act, h_ps, n + 1)
                    if not (isinstance(i, int) and n < 2):
                        wait_apart(act, lo_set, n - 1)
                    act.activation(act_full[:, u % 2, :], H1[:, u % 2, :], ACT.Gelu, bias=bias).then_inc(gelu_full, 1)
                    if not (isinstance(i, int) and n < SLOTS):
                        wait_apart(act, mm2, n - SLOTS + 1)
                    act.activation(act_hi[:, u % SLOTS, :], H1[:, u % 2, :], ACT.Gelu, bias=bias).then_inc(gelu_hi, 1)

                for u in range(2 * UE):
                    gelu(0, u)
                with act.Fori(1, E // 2) as i:
                    for u in range(2 * UE):
                        gelu(i, u)

            @block.vector
            def _(dve):
                def split(i, e):
                    if e == 0:
                        dve.wait_ge(w_in, 32 * (i + 1))
                    if not (isinstance(i, int) and i == 0):
                        dve.wait_ge(mm2, 2 * UE * (i - 1) + UE * (e + 1))
                    dve.tensor_copy(w1_hi[:, e, :], w1_raw[:, e, :]).then_inc(w_hi, 1)
                    dve.tensor_copy(w2_hi[:, e], w2_raw[:, e]).then_inc(w_hi, 1)
                    dve.wait_ge(w_hi, 4 * i + 2 * e + 1)
                    dve.tensor_tensor(w1_lo[:, e, :], w1_raw[:, e, :], w1_hi[:, e, :].bitcast(F32), ALU.subtract).then_inc(w_lo, 1)
                    dve.wait_ge(w_hi, 4 * i + 2 * e + 2)
                    dve.tensor_tensor(w2_lo[:, e], w2_raw[:, e], w2_hi[:, e].bitcast(F32), ALU.subtract).then_inc(w_lo, 1)

                split(0, 0)

                count = 0

                def then(ins):
                    nonlocal count
                    count += 1
                    ins.then_inc(step, 1)
                    dve.wait_ge(step, count)

                def wide(v):
                    return v.unsqueeze(2).to_broadcast([P, NT, E])

                lg, sel1, rest, sel2, tmp, keep, shifted, expd, kept = (pick[:, n] for n in range(9))
                then(dve.tensor_scalar(lg, logits[:], 1.0 / TEMP, None, ALU.mult))

                def largest(src, n, sel):
                    then(dve.tensor_reduce(top[:, n], src, AX.X, ALU.max))
                    then(dve.tensor_tensor(tmp, src, wide(top[:, n]), ALU.is_ge))
                    then(dve.tensor_tensor(tmp, tmp, order[:].unsqueeze(1).to_broadcast([P, NT, E]), ALU.mult))
                    then(dve.tensor_reduce(top[:, n + 1], tmp, AX.X, ALU.max))
                    then(dve.tensor_tensor(sel, tmp, wide(top[:, n + 1]), ALU.is_ge))

                dve.wait_ge(order_set, E)
                largest(lg, 0, sel1)
                dve.tensor_tensor(shifted, lg, wide(top[:, 0]), ALU.subtract).then_inc(masked_exp, 1)
                then(dve.scalar_tensor_tensor(out=rest, in0=sel1, scalar=LOWEST, in1=lg, op0=ALU.mult, op1=ALU.add))
                largest(rest, 2, sel2)
                then(dve.tensor_tensor(keep, sel1, sel2, ALU.add))
                dve.wait_ge(masked_exp, 2)
                then(dve.tensor_tensor(kept, expd, keep, ALU.mult))
                then(dve.tensor_reduce(top[:, 4], kept, AX.X, ALU.add))
                then(dve.reciprocal(top[:, 5], top[:, 4]))
                dve.tensor_tensor(gates[:], kept, wide(top[:, 5]), ALU.mult).then_inc(gates_set, 1)
                for n in range(4):
                    dve.wait_ge(gT_ps, n + 1)
                    if n < 3:
                        pass
                for n in range(4):
                    dve.tensor_copy(gatesT[:, n * 512:(n + 1) * 512], Y[0:E, n // 2, (n % 2) * 512:(n % 2 + 1) * 512]).then_inc(gT_set, 1)
                for n in range(4):
                    dve.wait_ge(bias_ps, n + 1)
                    dve.tensor_copy(acc[:, n * 512:(n + 1) * 512], Y[:, n // 2, (n % 2) * 512:(n % 2 + 1) * 512]).then_inc(acc_init, 1)

                def low(i, u):
                    n = 2 * UE * i + u
                    dve.wait_ge(gelu_hi, n + 1)
                    dve.wait_ge(gelu_full, n + 1)
                    if not (isinstance(i, int) and n < SLOTS):
                        dve.wait_ge(mm2, n - SLOTS + 1)
                    dve.tensor_tensor(act_lo[:, u % SLOTS, :], act_full[:, u % 2, :], act_hi[:, u % SLOTS, :].bitcast(F32),
                                      ALU.subtract).then_inc(lo_set, 1)

                def gate(i, g):
                    e, half = g // 2, g % 2
                    dve.wait_ge(mm2, 2 * UE * i + FC * (g + 1))
                    if half == 0:
                        dve.wait_ge(row_in[e], 16 * (i + 1))
                    if not (isinstance(i, int) and i == 0 and e == 0):
                        dve.wait_ge(acc_done, 4 * i + g - 1)
                    dve.tensor_tensor(gated[:, half, :], Y[:, half, :], gate_row[:, e, half * HALF:(half + 1) * HALF],
                                      ALU.mult).then_inc(gate_done, 1)

                def pair(i, first_pair=False, last_pair=False):
                    for u in range(2 * UE):
                        if u == UE // 2 and first_pair:
                            split(i, 1)
                        if u == UE // 2 + 1 and not first_pair:
                            split(i, 1)
                        if u == 2 * UE - 2 and not last_pair:
                            split(i + 1, 0)
                        low(i, u)
                        if u >= LAG + FC and (u - LAG) % FC == 0:
                            gate(i, (u - LAG) // FC - 1)
                        if u == LAG and not first_pair:
                            gate(i - 1, 3)

                pair(0, first_pair=True)
                with dve.Fori(1, E // 2 - 1) as i:
                    pair(i)
                pair(E // 2 - 1, last_pair=True)
                gate(E // 2 - 1, 3)

                for b in range(B):
                    dve.wait_ge(outT_ps, b + 1)
                    y = Y[:, b // 2, (b % 2) * 512:(b % 2 + 1) * 512].rearrange("p (t c) -> p t c", c=C)
                    for t in range(TT):
                        dve.bn_stats(stats[:, t, :], y[:, t, :]).then_inc(f_stat, 1)
                    for t in range(TT):
                        dve.wait_ge(f_stat, TT * b + t + 1)
                        dve.bn_aggr(mv[:, t, :], stats[:, t, :]).then_inc(f_aggr, 1)
                    dve.wait_ge(f_aggr, TT * b + TT)
                    dve.tensor_scalar(vare[:], mv[:, :, 1], EPS, None, ALU.add).then_inc(f_var, 1)
                    dve.wait_ge(f_rstd, b + 1)
                    o = outs[:, b % 2]
                    if b >= 2:
                        dve.wait_ge(stored, 16 * (b - 1))
                    for t in range(TT):
                        dve.tensor_scalar(o[:, t, :], y[:, t, :], mv[:, t, 0:1], rstd[:, t:t + 1],
                                          ALU.subtract, ALU.mult).then_inc(f_norm, 1)
                    dve.wait_ge(f_norm, TT * b + TT)
                    dve.tensor_tensor(o, o, gate_out[:, b:b + 1, :].to_broadcast([P, TT, C]), ALU.mult).then_inc(f_gated, 1)
                    dve.wait_ge(f_gated, b + 1)
                    dve.wait_ge(xo_set, b + 1)
                    dve.tensor_tensor(o, o, xs[:, b * TT:(b + 1) * TT, :], ALU.add).then_inc(f_out, 1)


_INS = ["L0_attn_x", "L0_attn_Wq", "L0_attn_bq", "L0_attn_Wk", "L0_attn_bk", "L0_attn_Wv", "L0_attn_bv",
        "L0_attn_Wo", "L0_attn_bo", "L0_attn_gamma", "L0_attn_beta", "L0_ffn_gate_w", "L0_ffn_gate_b",
        "L0_ffn_w1", "L0_ffn_b1", "L0_ffn_w2", "L0_ffn_b2", "L0_ffn_ln_g", "L0_ffn_ln_b", "L0_c", "L0_wmod"]


def kernel(**inputs):
    import numpy as np
    import concourse.bacc as bacc
    from concourse.bass_utils import run_bass_kernel_spmd

    nc = bacc.Bacc("TRN2", target_bir_lowering=False, num_devices=1)
    arrays, args = {}, []
    for name in _INS:
        a = np.ascontiguousarray(inputs[name])
        arrays[f"in_{name}"] = a
        args.append(nc.dram_tensor(f"in_{name}", a.shape, mybir.dt.from_np(a.dtype), kind="ExternalInput").ap())
    shape = inputs["L0_attn_x"].shape
    args.append(nc.dram_tensor("out_x", shape, F32, kind="ExternalOutput").ap())
    build(nc, *args)
    r = run_bass_kernel_spmd(nc, [arrays], core_ids=[0])
    return r.results[0]["out_x"]
```

```python
import math
from contextlib import ExitStack

import concourse.bass as bass
from concourse import mybir

F32 = mybir.dt.float32
F32R = mybir.dt.float32r
ALU = mybir.AluOpType
ACT = mybir.ActivationFunctionType
AX = mybir.AxisListType

P = 128
EPS = 1e-5
TEMP = 0.9
LOWEST = -3.0e38


def ds(i, n=1):
    return bass.ds(i, n)


def build(nc, x, wq, bq, wk, bk, wv, bv, wo, bo, gamma, beta, gate_w, gate_b, w1, b1, w2, b2,
          ln_g, ln_b, c, wmod, out):
    B, T, C = x.shape
    H, DH = 16, C // 16
    E, _, F = w1.shape
    TT = T // P
    NT = B * TT
    QUADS = H // 4
    FC = F // P
    N = B * T
    assert C == P and T == 512 and DH == 8 and FC == 4
    SCALE = float(DH) ** -0.5

    ROW_BQ, ROW_BK, ROW_C, NROWS = E * FC, E * FC + 1, E * FC + 2, E * FC + 2 + B

    Q_PIECE, K_PIECE = (0, 0, 1), (0, 1, 0)
    MAX_ROW = 3 * DH
    Q_ROWS = MAX_ROW + 2
    K_ROWS = P // 4
    ONE = 1

    FILLS = [[(0, 3, 0)], [(1, 3, 0)], [(0, 2, 0), (0, 0, 384)], [(1, 2, 0), (1, 0, 384)],
             [(2, 3, 0)], [(3, 3, 0)], [(2, 2, 0), (2, 0, 384)], [(3, 2, 0), (3, 0, 384)],
             [(0, 1, 0), (2, 1, 256)], [(1, 1, 0), (3, 1, 256)]]
    NFILL = len(FILLS)
    AFTER = []
    for f in range(NFILL):
        AFTER.append((AFTER[-1] if AFTER else 0) + len(FILLS[f]))
    NMAX = AFTER[-1]
    TURNS, SPLITS = [16, 22, 34], [16, 22, 33]
    LAST_TURN, LAST_SPLIT = 0, 2
    UNITS = [[(h, 0, 0)] for h in range(4)] + [[(h, 3, 0), (h, 1, 128)] for h in range(4)] + [
        [(0, 2, 0), (2, 2, 256)], [(1, 2, 0), (3, 2, 256)]]
    NU = len(UNITS)
    PLACE = {(h, ch): u * 512 + col for u, parts in enumerate(UNITS) for h, ch, col in parts}
    NS = NU // 2
    PV_ORDER = [(0, 1), (1, 3), (3, 3), (2, 4)]
    STEPS = QUADS * NFILL
    assert NU == NFILL
    BANKS = [s % 3 for s in range(STEPS - 1)]
    BANKS.append(3 - BANKS[0] - BANKS[-1])
    assert len(set(BANKS[-3:] + BANKS[:1])) == 3 and BANKS[-1] not in (BANKS[0], BANKS[-2])
    USED_BY = [max(r for r in range(-STEPS, s) if BANKS[r % STEPS] == BANKS[s]) for s in range(STEPS)]

    q_rows = nc.dram_tensor("q_rows", [B, H, Q_ROWS, T], F32)
    k_rows = nc.dram_tensor("k_rows", [B, H, K_ROWS, T], F32)
    gates_dram = nc.dram_tensor("gates_dram", [E, N], F32)

    x_v = x.rearrange("b (t p) c -> p (b t) c", p=P)
    out_v = out.rearrange("b (t p) c -> p (b t) c", p=P)
    w1_v = w1.rearrange("e d f -> d e f")
    w2_v = w2.rearrange("e (k f) d -> f e k d", f=P)

    def row(v):
        return v.rearrange("(o n) -> o n", o=1).to_broadcast([P, v.shape[0]])

    with ExitStack() as whole:
        def sem(name):
            return whole.enter_context(nc.semaphore(name))

        def shared(name, shape, dt=F32):
            return whole.enter_context(nc.sbuf_tensor(name, shape, dt))

        xs = shared("xs", [P, NT, C])
        ident = shared("ident", [P, P])
        cols = shared("cols", [P, NROWS])
        half_neg = shared("half_neg", [P, NT])
        gate_out = shared("gate_out", [P, B, C])
        bias_out = shared("bias_out", [P, B, C])
        h2_hi = shared("h2_hi", [P, N], F32R)
        h2_lo = shared("h2_lo", [P, N], F32R)
        logits = shared("logits", [P, NT, E])
        gate_b_all = shared("gate_b_all", [P, E])
        w1_raw = shared("w1_raw", [P, 2, F])
        w2_raw = shared("w2_raw", [P, 2, FC, C])
        b2_rows = shared("b2_rows", [E, C])
        w1_hi = shared("w1_hi", [P, 2, F], F32R)
        w1_lo = shared("w1_lo", [P, 2, F], F32R)

        w_in = sem("w_in")
        go = sem("go")
        w_hi, w_lo = sem("w_hi"), sem("w_lo")

        def wait_apart(eng, sem_, value):
            if not isinstance(value, int):
                value = eng.to_reg(value)
                eng.wait_ge(go, 1)
            eng.wait_ge(sem_, value)

        with ExitStack() as ctx:
            def sb(name, shape, dt=F32):
                return ctx.enter_context(nc.sbuf_tensor(name, shape, dt))

            def ps(name, shape):
                return ctx.enter_context(nc.psum_tensor(name, shape, F32))

            mask = sb("mask", [P, T])
            rows = sb("rows", [NROWS, P])
            wqs, wks, wvs, wos = (sb(n, [P, C]) for n in ("wqs", "wks", "wvs", "wos"))
            gws = sb("gws", [P, E])
            bv_all, bo_all, gam_all, bet_all, lng_all, lnb_all = (
                sb(n, [P, C]) for n in ("bv_all", "bo_all", "gam_all", "bet_all", "lng_all", "lnb_all"))
            sil = sb("sil", [P, 3, B])
            silu = sb("silu", [P, B])
            modc = sb("modc", [P, 4, B])
            gate_mid = sb("gate_mid", [P, B, C])
            bias_mid = sb("bias_mid", [P, B, C])
            stats = sb("stats", [P, TT, 6])
            mv = sb("mv", [P, TT, 2])
            vare = sb("vare", [P, TT])
            rstd = sb("rstd", [P, TT])
            norm = sb("norm", [P, TT, C])
            hT = sb("hT", [P, T])
            q_out = sb("q_out", [P, 2, T], F32R)
            k_out = sb("k_out", [P, 2, T], F32R)
            v_all = sb("v_all", [P, B, TT, C])
            v_pad = sb("v_pad", [P, TT, H, 32])
            qa = sb("qa", [P, 2, 4, T], F32R)
            ka = sb("ka", [P, 2, T], F32R)
            qb = sb("qb", [P, QUADS, 4, T], F32R)
            kb = sb("kb", [P, QUADS, T], F32R)
            junk = sb("junk", [P, 2, T])
            maxes = sb("maxes", [P, H * TT])
            max_out = sb("max_out", [4 * TT, QUADS, 2, P], F32R)
            probs = sb("probs", [P, 2, NU * 512])
            clamp = probs[:, 0, 0:8 * B * C].rearrange("p (n b c) -> p n b c", b=B, c=C)
            o_spread = sb("o_spread", [P, QUADS, T])
            wmods = probs[:, 0, 8 * B * C:(8 * B + 6) * C]
            silu_wide = probs[:, 1, 8 * T:8 * T + B * P].rearrange("p (b c) -> p b c", b=B)
            ys, o_norm = (q_out[:, n, :].bitcast(F32).rearrange("p (t c) -> p t c", t=TT) for n in range(2))
            k_tail = probs[0:B * H, 1, 0:(K_ROWS - MAX_ROW) * T]
            ones_row = sb("ones_row", [1, P])
            one = sb("one", [P, 1])
            rec = sb("rec", [P, TT, H])
            oT = sb("oT", [P, T])
            h2 = sb("h2", [P, T])

            S = ps("S", [P, 3, 512])
            X = ps("X", [P, 3, 512])
            O = ps("O", [P, 512])
            M = ps("M", [P, 512])

            KV = S[:, 1:3, :]
            FIRST_BANKS = 4

            def fill_bank(b, q, f):
                if isinstance(b, int) and b == 0:
                    n = (NFILL * q + f) % FIRST_BANKS
                    return X[:, n, :] if n < 3 else S[:, 0, :]
                return X[:, BANKS[NFILL * q + f], :]

            def head_bank(b, t):
                if isinstance(b, int) and b == B - 1:
                    return (X[:, 0, :], X[:, 1, :], X[:, 2, :], S[:, 0, :])[t]
                return M[:]

            gate_banks = (S[:, 0, :], X[:, 2, :])

            rows_in, mod_in, proj_in, bcast_in, late_in = map(sem, ("rows_in", "mod_in", "proj_in", "bcast_in", "late_in"))
            x_in, tail_saved = sem("x_in"), sem("tail_saved")
            ident_set, consts_set, mask_set = map(sem, ("ident_set", "consts_set", "mask_set"))
            tail_set, qa_zero, qb_zero = map(sem, ("tail_set", "qa_zero", "qb_zero"))
            cols_ps, cols_set = sem("cols_ps"), sem("cols_set")
            sil_exp, sil_step = sem("sil_exp"), sem("sil_step")
            mod_ps, gmid_ps, gout_ps, modc_set, gates_copied, clamped, modrow_set = map(
                sem, ("mod_ps", "gmid_ps", "gout_ps", "modc_set", "gates_copied", "clamped", "modrow_set"))
            row_set, twice_set, signed_set = map(sem, ("row_set", "twice_set", "signed_set"))
            x_stat, x_aggr, x_var, x_rstd, x_norm = map(sem, ("x_stat", "x_aggr", "x_var", "x_rstd", "x_norm"))
            xT_ps, hT_set, q_ps, k_ps, v_ps = map(sem, ("xT_ps", "hT_set", "q_ps", "k_ps", "v_ps"))
            q_hi, q_lo, k_hi, k_lo, v_set, qk_saved = map(sem, ("q_hi", "q_lo", "k_hi", "k_lo", "v_set", "qk_saved"))
            a_in = [sem(f"a_in{s}") for s in range(2)]
            b_in = [sem(f"b_in{q}") for q in range(QUADS)]
            fill_ps, rowmax, maxT_ps, max_hi, max_lo, max_saved = map(sem, ("fill_ps", "rowmax", "maxT_ps", "max_hi", "max_lo", "max_saved"))
            vpad_set, unit_ps, exps, masked, pv_ps, o_out = map(sem, ("vpad_set", "unit_ps", "exps", "masked", "pv_ps", "o_out"))
            oT1_ps, rec_set, onorm_set, oT2_ps, oT_set, y_ps, y_set = map(sem, ("oT1_ps", "rec_set", "onorm_set", "oT2_ps", "oT_set", "y_ps", "y_set"))
            y_stat, y_aggr, y_var, y_rstd, y_gated, xb_set, x1_set = map(sem, ("y_stat", "y_aggr", "y_var", "y_rstd", "y_gated", "xb_set", "x1_set"))
            r_stat, r_aggr, r_var, r_rstd, r_norm, rT_ps = map(sem, ("r_stat", "r_aggr", "r_var", "r_rstd", "r_norm", "rT_ps"))
            h2hi_set, h2_set, h2lo_set, lg_ps, lg_set = map(sem, ("h2hi_set", "h2_set", "h2lo_set", "lg_ps", "lg_set"))

            from_one = (x_in, hT_set, q_lo, k_lo, v_set, v_ps, qk_saved, x_norm, xT_ps,
                        exps, h2hi_set, h2_set, lg_set, o_out, oT1_ps, pv_ps, y_ps, oT2_ps, lg_ps, max_saved)

            block = ctx.enter_context(nc.Block())

            @block.sync
            def _(sp):
                sp.wait_ge(go, 1)
                def load_x(b):
                    if b > 0:
                        sp.wait_ge(x_in, ONE + 16 * b)
                    sp.dma_start(xs[:, TT * b:TT * (b + 1), :], x_v[:, TT * b:TT * (b + 1), :]).then_inc(x_in, 16)

                sp.dma_start(rows[0:E * FC, :], b1.rearrange("e (k f) -> (e k) f", f=P)).then_inc(rows_in, 16)
                sp.dma_start(rows[ROW_BQ:ROW_BQ + 1, :], bq.rearrange("(o n) -> o n", o=1)).then_inc(rows_in, 16)
                sp.dma_start(rows[ROW_BK:ROW_BK + 1, :], bk.rearrange("(o n) -> o n", o=1)).then_inc(rows_in, 16)
                sp.dma_start(rows[ROW_C:NROWS, :], c).then_inc(rows_in, 16)
                load_x(0)
                sp.dma_start(wmods[:], wmod).then_inc(mod_in, 16)
                for dst, src in ((wqs, wq), (wks, wk), (wvs, wv)):
                    sp.dma_start(dst[:], src).then_inc(proj_in, 16)
                load_x(1)
                for dst, src in ((bv_all, bv), (gam_all, gamma), (bet_all, beta), (lng_all, ln_g), (lnb_all, ln_b)):
                    sp.dma_start(dst[:], row(src)).then_inc(bcast_in, 16)
                sp.wait_ge(tail_set, 2)
                sp.dma_start(k_rows[:, :, MAX_ROW:K_ROWS, :].rearrange("b h r t -> (b h) (r t)"), k_tail).then_inc(tail_saved, 16)
                load_x(2)

                def save(b):
                    for done, src, dst, piece in ((q_lo, q_out, q_rows, Q_PIECE), (k_lo, k_out, k_rows, K_PIECE)):
                        sp.wait_ge(done, ONE + b + 1)
                        for r, half in enumerate(piece):
                            sp.dma_start(dst[b, :, DH * r:DH * (r + 1), :], src[:, half, :].bitcast(F32)).then_inc(qk_saved, 16)

                def quad_of(src, b, q):
                    return src[ds(b), 4 * q:4 * q + 4].rearrange("o h r t -> (o h) r t")

                def load_a(b, q):
                    if not (isinstance(b, int) and b == 0 and q < 2):
                        wait_apart(sp, fill_ps, NFILL * (QUADS * b + q - 1))
                    sp.dma_start(ka[:, q % 2, :].bitcast(F32), quad_of(k_rows, b, q).rearrange("h r t -> (h r) t")).then_inc(a_in[q % 2], 16)
                    for j in range(4):
                        sp.dma_start(qa[K_ROWS * j:K_ROWS * j + MAX_ROW, q % 2, j, :].bitcast(F32),
                                     quad_of(q_rows, b, q)[j, 0:MAX_ROW, :]).then_inc(a_in[q % 2], 16)

                def load_b(b, nxt, q):
                    if not (isinstance(b, int) and b == 0):
                        wait_apart(sp, unit_ps, NU * (QUADS * (b - 1) + q + 1))
                    sp.dma_start(kb[:, q, :].bitcast(F32), quad_of(k_rows, b, q).rearrange("h r t -> (h r) t")).then_inc(b_in[q], 16)
                    if q + 2 < QUADS:
                        load_a(b, q + 2)
                    elif nxt is not None:
                        load_a(nxt, q + 2 - QUADS)
                    if isinstance(b, int) and b == 0 and q + 2 < B:
                        save(q + 2)
                    wait_apart(sp, max_lo, QUADS * b + q + 1)
                    for half in range(2):
                        sp.dma_start(q_rows[ds(b), 4 * q:4 * q + 4, MAX_ROW + half].rearrange("o h (t p) -> (o h) t p", p=P),
                                     max_out[:, q, half, :].bitcast(F32)).then_inc(max_saved, 16)
                    wait_apart(sp, max_saved, ONE + 32 * (QUADS * b + q + 1))
                    for j in range(4):
                        sp.dma_start(qb[K_ROWS * j:K_ROWS * j + Q_ROWS, q, j, :].bitcast(F32),
                                     quad_of(q_rows, b, q)[j]).then_inc(b_in[q], 16)

                save(0)
                sp.wait_ge(tail_saved, 16)
                sp.wait_ge(qk_saved, ONE + 96)
                sp.wait_ge(qa_zero, 1)
                load_a(0, 0)
                load_a(0, 1)
                load_x(3)
                save(1)
                for dst, src in ((bo_all, row(bo)), (gate_b_all, row(gate_b)), (wos, wo), (gws, gate_w), (b2_rows, b2)):
                    sp.dma_start(dst[:], src).then_inc(late_in, 16)
                sp.wait_ge(qb_zero, 1)
                for q in range(QUADS):
                    if q == QUADS - 2:
                        sp.wait_ge(qk_saved, ONE + 96 * B)
                    load_b(0, 1, q)
                with sp.Fori(1, B - 1) as b:
                    for q in range(QUADS):
                        load_b(b, b + 1, q)
                for q in range(QUADS):
                    load_b(B - 1, None, q)
                sp.dma_start(w1_raw[:], w1_v[:, 0:2, :]).then_inc(w_in, 16)
                sp.dma_start(w2_raw[:], w2_v[:, 0:2, :, :]).then_inc(w_in, 16)

            @block.gpsimd
            def _(pool):
                pool.memset(ident[:], 0.0).then_inc(ident_set, 1)
                for s_ in from_one:
                    pool.sem_inc(s_, ONE)
                pool.sem_inc(go, 1)
                pool.wait_ge(ident_set, 1)
                pool.affine_select(out=ident[:], in_=ident[:], compare_op=ALU.not_equal, fill=1.0, base=0,
                                   pattern=[[-1, P]], channel_multiplier=1).then_inc(ident_set, 1)
                pool.memset(half_neg[:], -0.5).then_inc(consts_set, 1)
                pool.memset(ones_row[:], 1.0).then_inc(row_set, 1)
                pool.memset(one[:], 1.0).then_inc(row_set, 1)
                pool.memset(mask[:], 0.0).then_inc(mask_set, 1)
                pool.wait_ge(mask_set, 1)
                pool.affine_select(out=mask[:, T - P:T], in_=mask[:, T - P:T], compare_op=ALU.is_ge, fill=LOWEST, base=0,
                                   pattern=[[-1, P]], channel_multiplier=1).then_inc(mask_set, 1)
                pool.wait_ge(consts_set, 1)

                def inv_sqrt(var, done, b):
                    pool.wait_ge(var, b + 1)
                    pool.tensor_tensor(rstd[:], vare[:], half_neg[:, 0:TT], ALU.pow).then_inc(done, 1)

                inv_sqrt(x_var, x_rstd, 0)
                pool.memset(qa[:].bitcast(F32), 0.0).then_inc(qa_zero, 1)
                inv_sqrt(x_var, x_rstd, 1)
                pool.memset(qb[:].bitcast(F32), 0.0).then_inc(qb_zero, 1)
                with pool.Fori(2, B) as b:
                    inv_sqrt(x_var, x_rstd, b)
                pool.memset(v_pad[:], 0.0).then_inc(consts_set, 1)
                pool.wait_ge(consts_set, 2)
                pool.memset(v_pad[:, :, :, DH:DH + 1], 1.0).then_inc(consts_set, 1)
                pool.wait_ge(row_set, 2)
                pool.wait_ge(gates_copied, 2)
                pool.wait_ge(bcast_in, 80)
                for n in range(2):
                    g, twice, sign, size = (clamp[:, 4 * n + k] for k in range(4))
                    pool.wait_ge(twice_set, n + 1)
                    pool.tensor_tensor(sign, twice, one[:].unsqueeze(2).to_broadcast([P, B, C]), ALU.subtract).then_inc(clamped, 1)
                    pool.wait_ge(clamped, 2 * n + 1)
                    pool.tensor_tensor(size, g, sign, ALU.mult).then_inc(clamped, 1)
                for n, (wt, bs, g_dst, b_dst) in enumerate(((gam_all, bet_all, gate_mid, bias_mid),
                                                            (lng_all, lnb_all, gate_out, bias_out))):
                    signed = clamp[:, 4 * n + 1]
                    pool.wait_ge(signed_set, n + 1)
                    pool.tensor_tensor(g_dst[:], signed, wt[:].unsqueeze(1).to_broadcast([P, B, C]), ALU.mult).then_inc(modrow_set, 1)
                    pool.tensor_tensor(b_dst[:], signed, bs[:].unsqueeze(1).to_broadcast([P, B, C]), ALU.mult).then_inc(modrow_set, 1)

                def select(b, q, u):
                    wait_apart(pool, exps, ONE + NU * (QUADS * b + q) + 2 * u + 2)
                    if u < 2:
                        v = probs[:, q % 2, ds(u * 1024, 1024)].rearrange("p (h c) -> p h c", h=2)[:, :, 0:P]
                        pattern = [[0, 2], [1, P]]
                    elif u < 4:
                        v = probs[:, q % 2, ds(u * 1024, 1024)].rearrange("p (h c) -> p h c", h=2)[:, :, 0:2 * P]
                        pattern = [[0, 2], [0, 2], [1, P]]
                    else:
                        v = probs[:, q % 2, ds(u * 1024, 1024)].rearrange("p (h c) -> p h c", h=4)[:, :, 0:P]
                        pattern = [[0, 4], [1, P]]
                    pool.affine_select(out=v, in_=v, compare_op=ALU.is_ge, fill=0.0, base=0,
                                       pattern=pattern, channel_multiplier=-1).then_inc(masked, 1)

                def residual(b):
                    pool.tensor_tensor(xs[:, ds(TT * b, TT), :], xs[:, ds(TT * b, TT), :],
                                       bias_mid[:, ds(b), :].to_broadcast([P, TT, C]), ALU.add).then_inc(xb_set, 1)

                def body(b, prev):
                    for q in range(QUADS):
                        for u in range(NS):
                            select(b, q, u)
                            if prev is not None:
                                if (q, u) == (0, 4):
                                    residual(prev)
                                if (q, u) == (2, 0):
                                    inv_sqrt(y_var, y_rstd, prev)
                                if (q, u) == (2, 3):
                                    inv_sqrt(r_var, r_rstd, prev)

                pool.wait_ge(modrow_set, 4)
                pool.wait_ge(x_norm, ONE + NT)
                body(0, None)
                with pool.Fori(1, B - 1) as b:
                    body(b, b - 1)
                body(B - 1, B - 2)
                residual(B - 1)
                inv_sqrt(y_var, y_rstd, B - 1)
                inv_sqrt(r_var, r_rstd, B - 1)

            @block.tensor
            def _(pe):
                pe.wait_ge(go, 1)
                pe.wait_ge(ident_set, 2)
                pe.wait_ge(rows_in, 64)
                pe.transpose(M[:, 0:NROWS], rows[:], ident[0:NROWS, 0:NROWS]).then_inc(cols_ps, 1)
                pe.wait_ge(sil_step, 4)
                pe.wait_ge(mod_in, 16)
                for n, j in enumerate((0, 1, 3, 4)):
                    mm = pe.matmul(O[:, n * B:(n + 1) * B], wmods[:, j * C:(j + 1) * C], silu[:], start=True, stop=True)
                mm.then_inc(mod_ps, 1)
                pe.wait_ge(proj_in, 48)
                pe.wait_ge(cols_set, 1)
                pe.wait_ge(modc_set, 2)

                def turn_x(b):
                    pe.wait_ge(x_norm, ONE + TT * b + TT)
                    pe.wait_ge(hT_set, ONE + b)
                    if b >= 3:
                        pe.wait_ge(max_lo, b - 2)
                    for t in range(TT):
                        mm = pe.transpose(M[:, t * P:(t + 1) * P], norm[:, t, :], ident[:])
                    mm.then_inc(xT_ps, 1)

                def project_q(b):
                    pe.wait_ge(hT_set, ONE + b + 1)
                    pe.wait_ge(q_lo, ONE + b)
                    pe.matmul(O[:], wqs[:], hT[:], start=True, stop=True).then_inc(q_ps, 1)

                def project_k(b):
                    pe.wait_ge(k_lo, ONE + b)
                    pe.matmul(KV[:, 0, :], wks[:], hT[:], start=True, stop=True).then_inc(k_ps, 1)

                def project_v(b):
                    pe.wait_ge(v_set, ONE + b)
                    if b == 0:
                        pe.wait_ge(row_set, 2)
                        pe.wait_ge(bcast_in, 80)
                    for t in range(TT):
                        pe.matmul(KV[:, 1, t * C:(t + 1) * C], hT[:, t * P:(t + 1) * P], wvs[:], start=True, stop=False)
                        mm = pe.matmul(KV[:, 1, t * C:(t + 1) * C], ones_row[:], bv_all[0:1, :], start=False, stop=True)
                    mm.then_inc(v_ps, 1)

                def rowmax_fill(b, q, f):
                    if f == 0:
                        pe.wait_ge(a_in[q % 2], 80 * (2 * b + q // 2 + 1))
                    if isinstance(b, int) and b == 0:
                        before = NFILL * q + f - FIRST_BANKS
                        if before >= 0:
                            pe.wait_ge(rowmax, NMAX * (before // NFILL) + AFTER[before % NFILL])
                        if NFILL * q + f == 2:
                            pe.wait_ge(gates_copied, 2)
                    else:
                        before = USED_BY[NFILL * q + f]
                        pe.wait_ge(rowmax, NMAX * (QUADS * b + before // NFILL) + AFTER[before % NFILL])
                    for head, tile, col in FILLS[f]:
                        mm = pe.matmul(fill_bank(b, q, f)[:, col:col + P * (tile + 1)], qa[:, q % 2, head, tile * P:(tile + 1) * P],
                                       ka[:, q % 2, 0:P * (tile + 1)], start=True, stop=True, skip_group_check=True)
                    mm.then_inc(fill_ps, 1)

                def max_turn(b, q):
                    pe.wait_ge(rowmax, NMAX * (QUADS * b + q + 1))
                    pe.wait_ge(max_lo, QUADS * b + q)
                    if isinstance(b, int) and b == 0:
                        pe.wait_ge(hT_set, ONE + min(q + 3, B))
                    elif not (isinstance(b, int) and b == 1):
                        ended = b - 2
                        if q == 0:
                            pe.wait_ge(oT_set, ended + 1)
                        elif q == 1:
                            pe.wait_ge(y_set, ended + 1)
                        elif q == 2:
                            pe.wait_ge(h2_set, ONE + ended + 1)
                        else:
                            pe.wait_ge(lg_set, ONE + ended + 1)
                    pe.transpose(M[0:4 * TT, 0:P], maxes[:, 4 * TT * q:4 * TT * (q + 1)], ident[:]).then_inc(maxT_ps, 1)

                def scores(b, q, u):
                    if u == 0:
                        pe.wait_ge(b_in[q], 80 * (b + 1))
                    before = USED_BY[NU * q + u]
                    if not (isinstance(b, int) and b == 0 and before < 0):
                        pe.wait_ge(exps, ONE + NU * QUADS * b + before + 1)
                    for head, ch, col in UNITS[u]:
                        mm = pe.matmul(S[:, BANKS[NU * q + u], col:col + T - P * ch], kb[:, q, ch * P:(ch + 1) * P],
                                       qb[:, q, head, ch * P:T], start=True, stop=True, skip_group_check=True)
                    mm.then_inc(unit_ps, 1)

                def values(b, q, n):
                    ch, select = PV_ORDER[n]
                    if n == 0:
                        if q == 0:
                            pe.wait_ge(vpad_set, b + 1)
                        pe.wait_ge(o_out, ONE + QUADS * b + q)
                    pe.wait_ge(masked, NS * (QUADS * b + q) + select + 1)
                    for j in range(4):
                        at = PLACE[j, ch]
                        mm = pe.matmul(O[32 * j:32 * j + 32, ch * P:T], v_pad[:, ch, 4 * q + j, :],
                                       probs[:, q % 2, at:at + T - P * ch], start=(n == 0), stop=(n == TT - 1),
                                       tile_position=(0, 32 * j), skip_group_check=True)
                    if n == TT - 1:
                        mm.then_inc(pv_ps, 1)

                def end_heads(b, t, nxt):
                    if t == 0:
                        pe.wait_ge(o_out, ONE + QUADS * b + QUADS)
                    if isinstance(b, int) and b == B - 1:
                        if t == 3:
                            pe.wait_ge(exps, ONE + NU * QUADS * B)
                    elif t == 0:
                        pe.wait_ge(max_lo, QUADS * (b + 2))
                    else:
                        pe.wait_ge(onorm_set, TT * b + t)
                    for q in range(QUADS):
                        mm = pe.transpose(head_bank(b, t)[:, q * P:(q + 1) * P], o_spread[:, q, t * P:(t + 1) * P], ident[:])
                    mm.then_inc(oT1_ps, 1)

                def end_turn(b):
                    if isinstance(b, int) and b == B - 1:
                        pe.wait_ge(lg_set, ONE + b)
                    for t in range(TT):
                        pe.wait_ge(onorm_set, TT * b + (t + 1 if isinstance(b, int) and b == B - 1 else TT))
                        mm = pe.transpose(M[:, t * P:(t + 1) * P], o_norm[:, t, :], ident[:])
                    mm.then_inc(oT2_ps, 1)

                def end_project(b, nxt):
                    pe.wait_ge(oT_set, b + 1)
                    if nxt is not None:
                        pe.wait_ge(max_lo, QUADS * nxt + 1)
                    for t in range(TT):
                        pe.matmul(M[:, t * C:(t + 1) * C], oT[:, t * P:(t + 1) * P], wos[:], start=True, stop=False)
                        mm = pe.matmul(M[:, t * C:(t + 1) * C], ones_row[:], bo_all[0:1, :], start=False, stop=True)
                    mm.then_inc(y_ps, 1)

                def end_turn_x(b, nxt):
                    if nxt is not None:
                        pe.wait_ge(max_lo, QUADS * nxt + 2)
                    for t in range(TT):
                        pe.wait_ge(r_norm, TT * b + t + 1)
                        mm = pe.transpose(M[:, t * P:(t + 1) * P], norm[:, t, :], ident[:])
                    mm.then_inc(rT_ps, 1)

                def end_logits(b, nxt):
                    pe.wait_ge(h2_set, ONE + b + 1)
                    if nxt is not None:
                        pe.wait_ge(max_lo, QUADS * nxt + 3)
                    for t in range(TT):
                        mm = pe.matmul(M[:, t * E:(t + 1) * E], h2[:, t * P:(t + 1) * P], gws[:], start=True, stop=True)
                    mm.then_inc(lg_ps, 1)

                def end_step(b, s, nxt):
                    if s in [6, 8, 10, 12]:
                        end_heads(b, [6, 8, 10, 12].index(s), nxt)
                    elif s == 14:
                        end_turn(b)
                    elif s == 19:
                        end_project(b, nxt)
                    elif s == 30:
                        end_turn_x(b, nxt)
                    elif s == 36:
                        end_logits(b, nxt)

                def body(b, prev, nxt):
                    for q in range(QUADS):
                        for f in range(NFILL):
                            s = NFILL * q + f
                            scores(b, q, f)
                            if nxt is not None:
                                rowmax_fill(nxt, q, f)
                                if s in TURNS:
                                    max_turn(nxt, TURNS.index(s))
                            if prev is not None:
                                if s < TT:
                                    values(prev, QUADS - 1, s)
                                if s == LAST_TURN:
                                    max_turn(b, QUADS - 1)
                                end_step(prev, s, nxt)
                            if f % 2 == 1 and f < 9 and q >= 1:
                                values(b, q - 1, f // 2)

                turn_x(0)
                project_q(0)
                project_k(0)
                project_v(0)
                turn_x(1)
                for j, bank, done in ((2, gate_banks[0], gmid_ps), (5, gate_banks[1], gout_ps)):
                    for b in range(B):
                        mm = pe.matmul(bank[:, b * C:(b + 1) * C], silu_wide[:, b, :], wmods[:, j * C:(j + 1) * C],
                                       start=True, stop=True)
                    mm.then_inc(done, 1)
                project_q(1)
                project_k(1)
                project_v(1)
                for q in range(QUADS):
                    for f in range(NFILL):
                        rowmax_fill(0, q, f)
                        if f == 5 and q >= 1:
                            max_turn(0, q - 1)
                        if f == 8 and q + 2 < B:
                            turn_x(q + 2)
                        if 0 < q < B - 1:
                            if f == 0:
                                project_q(q + 1)
                            if f == 3:
                                project_k(q + 1)
                            if f == 4:
                                project_v(q + 1)
                max_turn(0, QUADS - 1)
                pe.wait_ge(q_lo, ONE + B)
                pe.wait_ge(k_lo, ONE + B)
                pe.wait_ge(v_set, ONE + B)
                pe.wait_ge(rowmax, NMAX * QUADS)
                pe.wait_ge(consts_set, 3)
                pe.wait_ge(late_in, 80)
                body(0, None, 1)
                with pe.Fori(1, B - 1) as b:
                    body(b, b - 1, b + 1)
                body(B - 1, B - 2, None)
                for n in range(TT):
                    values(B - 1, QUADS - 1, n)
                for s in range(QUADS * NFILL):
                    end_step(B - 1, s, None)

            @block.scalar
            def _(act):
                act.wait_ge(go, 1)
                act.wait_ge(cols_ps, 1)
                act.activation(cols[:], M[:, 0:NROWS], ACT.Copy).then_inc(cols_set, 1)
                act.wait_ge(cols_set, 1)
                act.activation(sil[:, 0, :], cols[:, ROW_C:ROW_C + B], ACT.Exp, scale=-1.0).then_inc(sil_exp, 1)

                def project(b):
                    act.wait_ge(modc_set, 2)
                    wait_apart(act, xT_ps, ONE + b + 1)
                    wait_apart(act, v_ps, ONE + b)
                    act.activation(hT[:], M[:], ACT.Identity, scale=modc[:, 1, ds(b)], bias=modc[:, 0, ds(b)]).then_inc(hT_set, 1)
                    act.wait_ge(qk_saved, ONE + 96 * b)
                    act.wait_ge(q_ps, b + 1)
                    act.activation(q_out[:, 0, :], O[:], ACT.Identity, bias=cols[:, ROW_BQ:ROW_BQ + 1]).then_inc(q_hi, 1)
                    act.wait_ge(k_ps, b + 1)
                    act.activation(k_out[:, 0, :], KV[:, 0, :], ACT.Identity, bias=cols[:, ROW_BK:ROW_BK + 1]).then_inc(k_hi, 1)
                    wait_apart(act, v_ps, ONE + b + 1)
                    act.activation(v_all[:, ds(b), :, :].rearrange("p o t c -> p (o t) c"),
                                   KV[:, 1, :].rearrange("p (t c) -> p t c", c=C), ACT.Copy).then_inc(v_set, 1)

                project(0)
                for n, done in enumerate((gmid_ps, gout_ps)):
                    act.wait_ge(done, 1)
                    act.activation(clamp[:, 4 * n], gate_banks[n].rearrange("p (b c) -> p b c", c=C), ACT.Copy).then_inc(gates_copied, 1)
                with act.Fori(1, B) as b:
                    project(b)

                def o_copy(b, q):
                    act.wait_ge(pv_ps, ONE + QUADS * b + q + 1)
                    if q == 0:
                        act.wait_ge(oT1_ps, ONE + TT * b)
                    act.activation(o_spread[:, q, :], O[:], ACT.Copy).then_inc(o_out, 1)

                def spread_v(b):
                    wait_apart(act, pv_ps, ONE + QUADS * b)
                    act.activation(v_pad[:, :, :, 0:DH], v_all[:, ds(b), :, :].rearrange("p o t (h i) -> p (o t) h i", i=DH),
                                   ACT.Copy).then_inc(vpad_set, 1)

                def end_turn(b):
                    act.wait_ge(oT2_ps, ONE + b + 1)
                    act.wait_ge(y_ps, ONE + b)
                    act.activation(oT[:], M[:], ACT.Copy).then_inc(oT_set, 1)

                def end_project(b):
                    act.wait_ge(y_ps, ONE + b + 1)
                    act.activation(ys[:], M[:].rearrange("p (t c) -> p t c", c=C), ACT.Copy).then_inc(y_set, 1)

                def end_h2(b):
                    wait_apart(act, rT_ps, b + 1)
                    act.activation(h2_hi[:, ds(T * b, T)], M[:], ACT.Identity, scale=modc[:, 3, ds(b)],
                                   bias=modc[:, 2, ds(b)]).then_inc(h2hi_set, 1)
                    wait_apart(act, lg_ps, ONE + b)
                    act.activation(h2[:], M[:], ACT.Identity, scale=modc[:, 3, ds(b)], bias=modc[:, 2, ds(b)]).then_inc(h2_set, 1)

                def body(b, prev):
                    for q in range(QUADS):
                        if q >= 1:
                            act.wait_ge(pv_ps, ONE + QUADS * b + q - 1)
                        for u in range(NU):
                            act.wait_ge(unit_ps, NU * (QUADS * b + q) + u + 1)
                            act.activation(probs[:, q % 2, u * 512:(u + 1) * 512], S[:, BANKS[NU * q + u], :],
                                           ACT.Exp, scale=SCALE).then_inc(exps, 1)
                            if (q, u) == (0, 3):
                                if prev is not None:
                                    o_copy(prev, QUADS - 1)
                                spread_v(b)
                            if prev is not None:
                                if (q, u) == (1, 5):
                                    end_turn(prev)
                                if (q, u) == (1, 9):
                                    end_project(prev)
                                if (q, u) == (3, 1):
                                    end_h2(prev)
                            if u == 7 and q >= 1:
                                o_copy(b, q - 1)

                act.wait_ge(v_set, ONE + B)
                act.wait_ge(modrow_set, 4)
                act.wait_ge(consts_set, 3)
                body(0, None)
                with act.Fori(1, B - 1) as b:
                    body(b, b - 1)
                body(B - 1, B - 2)
                o_copy(B - 1, QUADS - 1)
                end_turn(B - 1)
                end_project(B - 1)
                end_h2(B - 1)

            @block.vector
            def _(dve):
                dve.wait_ge(go, 1)
                dve.memset(k_tail[:, 0:2 * T], 1.0).then_inc(tail_set, 1)
                dve.memset(k_tail[:, 2 * T:], 0.0).then_inc(tail_set, 1)

                def layer_stats(src, stat, aggr, var, b):
                    for t in range(TT):
                        dve.bn_stats(stats[:, t, :], src(t)).then_inc(stat, 1)
                    for t in range(TT):
                        wait_apart(dve, stat, TT * b + t + 1)
                        dve.bn_aggr(mv[:, t, :], stats[:, t, :]).then_inc(aggr, 1)
                    dve.wait_ge(aggr, TT * b + TT)
                    dve.tensor_scalar(vare[:], mv[:, :, 1], EPS, None, ALU.add).then_inc(var, 1)

                def normalise(src, dst, rs, done, b):
                    dve.wait_ge(rs, b + 1)
                    for t in range(TT):
                        dve.tensor_scalar(dst[:, t, :], src(t), mv[:, t, 0:1], rstd[:, t:t + 1],
                                          ALU.subtract, ALU.mult).then_inc(done, 1)

                def tile_of_x(b):
                    return lambda t: xs[:, ds(TT * b + t), :].rearrange("p o c -> p (o c)")

                def x_stats(b):
                    dve.wait_ge(x_in, ONE + 16 * b + 16)
                    wait_apart(dve, x_norm, ONE + TT * b)
                    layer_stats(tile_of_x(b), x_stat, x_aggr, x_var, b)

                def project_low(b):
                    dve.wait_ge(q_hi, b + 1)
                    dve.scalar_tensor_tensor(out=q_out[:, 1, :], in0=O[:], scalar=cols[:, ROW_BQ:ROW_BQ + 1],
                                             in1=q_out[:, 0, :].bitcast(F32), op0=ALU.add, op1=ALU.subtract).then_inc(q_lo, 1)
                    dve.wait_ge(k_hi, b + 1)
                    dve.scalar_tensor_tensor(out=k_out[:, 1, :], in0=KV[:, 0, :], scalar=cols[:, ROW_BK:ROW_BK + 1],
                                             in1=k_out[:, 0, :].bitcast(F32), op0=ALU.add, op1=ALU.subtract).then_inc(k_lo, 1)

                def normalise_x(b):
                    dve.wait_ge(xT_ps, ONE + b)
                    normalise(tile_of_x(b), norm, x_rstd, x_norm, b)

                x_stats(0)
                dve.wait_ge(sil_exp, 1)
                dve.tensor_scalar(sil[:, 1, :], sil[:, 0, :], 1.0, None, ALU.add).then_inc(sil_step, 1)
                dve.wait_ge(sil_step, 1)
                dve.reciprocal(sil[:, 2, :], sil[:, 1, :]).then_inc(sil_step, 1)
                dve.wait_ge(sil_step, 2)
                dve.tensor_tensor(silu[:], cols[:, ROW_C:ROW_C + B], sil[:, 2, :], ALU.mult).then_inc(sil_step, 1)
                dve.wait_ge(sil_step, 3)
                dve.tensor_copy(silu_wide[:], silu[:].unsqueeze(2).to_broadcast([P, B, P])).then_inc(sil_step, 1)
                normalise_x(0)
                dve.wait_ge(mod_ps, 1)
                mods = O[:, 0:4 * B].rearrange("p (n b) -> p n b", b=B)
                dve.tensor_copy(modc[:, 0:4:2, :], mods[:, 0:4:2, :]).then_inc(modc_set, 1)
                dve.tensor_scalar(modc[:, 1:4:2, :], mods[:, 1:4:2, :], 1.0, None, ALU.add).then_inc(modc_set, 1)

                x_stats(1)
                project_low(0)
                normalise_x(1)
                x_stats(2)
                project_low(1)
                dve.wait_ge(gates_copied, 2)
                for n in range(2):
                    dve.tensor_scalar(clamp[:, 4 * n + 1], clamp[:, 4 * n], 0.0, 2.0, ALU.is_ge, ALU.mult).then_inc(twice_set, 1)

                def max_fill(b, q, f):
                    wait_apart(dve, fill_ps, NFILL * (QUADS * b + q) + f + 1)
                    k = AFTER[f] - len(FILLS[f])
                    for n, (head, tile, col) in enumerate(FILLS[f]):
                        if not (isinstance(b, int) and b == 0 and q == 0 and k + n < 2):
                            wait_apart(dve, rowmax, NMAX * (QUADS * b + q) + k + n - 1)
                        width = P * (tile + 1)
                        at = TT * (4 * q + head) + tile
                        dve.tensor_tensor_reduce(out=junk[:, (k + n) % 2, 0:width], in0=fill_bank(b, q, f)[:, col:col + width],
                                                 in1=mask[:, T - width:T], scale=1.0, scalar=LOWEST, op0=ALU.add,
                                                 op1=ALU.max, accum_out=maxes[:, at:at + 1]).then_inc(rowmax, 1)

                def max_split(b, q):
                    dve.wait_ge(maxT_ps, QUADS * b + q + 1)
                    dve.wait_ge(max_saved, ONE + 32 * QUADS * b)
                    turned = M[0:4 * TT, 0:P]
                    dve.tensor_scalar(max_out[:, q, 0, :], turned, -1.0, None, ALU.mult).then_inc(max_hi, 1)
                    dve.wait_ge(max_hi, QUADS * b + q + 1)
                    dve.scalar_tensor_tensor(out=max_out[:, q, 1, :], in0=turned, scalar=-1.0, in1=max_out[:, q, 0, :].bitcast(F32),
                                             op0=ALU.mult, op1=ALU.subtract).then_inc(max_lo, 1)

                def end_divide(b, t):
                    dve.wait_ge(oT1_ps, ONE + TT * b + t + 1)
                    o = head_bank(b, t).rearrange("p (h i) -> p h i", i=32)
                    dve.reciprocal(rec[:, t, :], o[:, :, DH]).then_inc(rec_set, 1)
                    dve.wait_ge(rec_set, TT * b + t + 1)
                    dve.wait_ge(oT2_ps, ONE + b)
                    dve.tensor_tensor(o_norm[:, t, :].rearrange("p (h i) -> p h i", i=DH), o[:, :, 0:DH],
                                      rec[:, t, :].unsqueeze(2).to_broadcast([P, H, DH]), ALU.mult).then_inc(onorm_set, 1)

                def end_stats_y(b):
                    wait_apart(dve, y_set, b + 1)
                    layer_stats(lambda t: ys[:, t, :], y_stat, y_aggr, y_var, b)

                def end_gate_y(b):
                    for t in range(TT):
                        dve.scalar_tensor_tensor(out=ys[:, t, :], in0=ys[:, t, :], scalar=mv[:, t, 0:1],
                                                 in1=gate_mid[:, ds(b), :].rearrange("p o c -> p (o c)"),
                                                 op0=ALU.subtract, op1=ALU.mult).then_inc(y_gated, 1)

                def end_residual(b):
                    wait_apart(dve, y_rstd, b + 1)
                    wait_apart(dve, xb_set, b + 1)
                    for t in range(TT):
                        wait_apart(dve, y_gated, TT * b + t + 1)
                        dve.scalar_tensor_tensor(out=tile_of_x(b)(t), in0=ys[:, t, :], scalar=rstd[:, t:t + 1],
                                                 in1=tile_of_x(b)(t), op0=ALU.mult, op1=ALU.add).then_inc(x1_set, 1)

                def end_stats_x(b):
                    wait_apart(dve, x1_set, TT * b + TT)
                    layer_stats(tile_of_x(b), r_stat, r_aggr, r_var, b)

                def end_norm_x(b):
                    normalise(tile_of_x(b), norm, r_rstd, r_norm, b)

                def end_h2_low(b):
                    dve.wait_ge(h2_set, ONE + b + 1)
                    dve.tensor_tensor(h2_lo[:, ds(T * b, T)], h2[:], h2_hi[:, ds(T * b, T)].bitcast(F32), ALU.subtract).then_inc(h2lo_set, 1)

                def end_logits(b):
                    dve.wait_ge(lg_ps, ONE + b + 1)
                    dve.tensor_tensor(logits[:, ds(TT * b, TT), :], M[:, 0:TT * E].rearrange("p (t e) -> p t e", e=E),
                                      gate_b_all[:].unsqueeze(1).to_broadcast([P, TT, E]), ALU.add).then_inc(lg_set, 1)

                END_STEPS = {19: end_stats_y, 20: end_gate_y, 22: end_residual, 24: end_stats_x,
                             27: end_norm_x, 32: end_h2_low, 37: end_logits}

                def end_step(b, s):
                    if s in [6, 8, 10, 12]:
                        end_divide(b, [6, 8, 10, 12].index(s))
                    elif s in END_STEPS:
                        END_STEPS[s](b)

                def body(b, prev, nxt):
                    for s in range(QUADS * NFILL):
                        if nxt is not None:
                            max_fill(nxt, s // NFILL, s % NFILL)
                        if prev is not None:
                            if s == LAST_SPLIT:
                                max_split(b, QUADS - 1)
                            end_step(prev, s)
                        if nxt is not None and s in SPLITS:
                            max_split(nxt, SPLITS.index(s))

                dve.wait_ge(mask_set, 2)
                for q in range(QUADS):
                    for f in range(NFILL):
                        max_fill(0, q, f)
                        if f == 5 and q >= 1:
                            max_split(0, q - 1)
                        if f == 3 and q + 2 < B:
                            normalise_x(q + 2)
                        if f == 4 and q == 2:
                            for n in range(2):
                                dve.wait_ge(clamped, 2 * n + 2)
                                dve.scalar_tensor_tensor(out=clamp[:, 4 * n + 1], in0=clamp[:, 4 * n + 3], scalar=0.25,
                                                         in1=clamp[:, 4 * n + 2], op0=ALU.max, op1=ALU.mult).then_inc(signed_set, 1)
                        if f == 6 and q + 3 < B:
                            x_stats(q + 3)
                        if f == 2 and 0 < q < B - 1:
                            project_low(q + 1)
                max_split(0, QUADS - 1)
                dve.wait_ge(modrow_set, 4)
                dve.wait_ge(late_in, 80)
                body(0, None, 1)
                with dve.Fori(1, B - 1) as b:
                    body(b, b - 1, b + 1)
                body(B - 1, B - 2, None)
                dve.wait_ge(w_in, 32)
                dve.tensor_copy(w1_hi[:, 0, :], w1_raw[:, 0, :]).then_inc(w_hi, 1)
                dve.wait_ge(w_hi, 1)
                dve.tensor_tensor(w1_lo[:, 0, :], w1_raw[:, 0, :], w1_hi[:, 0, :].bitcast(F32), ALU.subtract).then_inc(w_lo, 1)
                for s in range(QUADS * NFILL):
                    end_step(B - 1, s)

        with ExitStack() as ctx:
            def sb(name, shape, dt=F32):
                return ctx.enter_context(nc.sbuf_tensor(name, shape, dt))

            def ps(name, shape):
                return ctx.enter_context(nc.psum_tensor(name, shape, F32))

            HALF = N // 2
            UE = 2 * FC
            LAG = 3
            SLOTS = 4

            w2_hi = sb("w2_hi", [P, 2, FC, C], F32R)
            w2_lo = sb("w2_lo", [P, 2, FC, C], F32R)
            act_full = sb("act_full", [P, 2, HALF])
            act_hi = sb("act_hi", [P, SLOTS, HALF], F32R)
            act_lo = sb("act_lo", [P, SLOTS, HALF], F32R)
            gate_row = sb("gate_row", [P, 2, N])
            gated = sb("gated", [P, 2, HALF])
            acc = sb("acc", [P, N])
            order = sb("order", [P, E])
            euler = sb("euler", [P, NT])
            top = sb("top", [P, 9, NT])
            pick = sb("pick", [P, 6, NT, E])
            gates = sb("gates", [P, NT, E])
            b2_cols = sb("b2_cols", [P, E])
            gates_turned = sb("gates_turned", [NT * E, P])
            stats = sb("o_stats", [P, TT, 6])
            mv = sb("o_mv", [P, B, TT, 2])
            neg_mean = sb("o_neg_mean", [P, B, TT])
            vare = sb("o_vare", [P, B, TT])
            rstd = sb("o_rstd", [P, B, TT])
            outs = sb("outs", [P, B, TT, C])
            H1 = ps("H1", [P, 2, HALF])
            Y = ps("Y", [P, 2, HALF])

            order_set, step, below_set, below_exp, gates_set = map(sem, ("order_set", "step", "below_set", "below_exp", "gates_set"))
            gT_ps, gT_set, gates_saved = map(sem, ("gT_ps", "gT_set", "gates_saved"))
            row_in = [sem(f"row_in{s}") for s in range(2)]
            h_ps, gelu_full, gelu_hi, lo_set = map(sem, ("h_ps", "gelu_full", "gelu_hi", "lo_set"))
            mm2, gate_done, acc_done = map(sem, ("mm2", "gate_done", "acc_done"))
            xo_set, outT_ps, f_stat, f_aggr, f_mean, f_var, f_rstd, f_centred, f_gated, f_gated_last, f_out, stored = map(
                sem, ("xo_set", "outT_ps", "f_stat", "f_aggr", "f_mean", "f_var", "f_rstd", "f_centred", "f_gated", "f_gated_last", "f_out", "stored"))

            block = ctx.enter_context(nc.Block())

            @block.sync
            def _(sp):
                sp.wait_ge(gT_set, 1)
                sp.dma_start(gates_dram[:].rearrange("e (t p) -> t e p", p=P), gates_turned[:]).then_inc(gates_saved, 16)
                sp.wait_ge(gates_saved, 16)

                def load_row(e, slot):
                    sp.dma_start(gate_row[:, slot, :], gates_dram[ds(e)].to_broadcast([P, N])).then_inc(row_in[slot], 16)

                for slot in range(2):
                    load_row(slot, slot)

                with sp.Fori(0, E // 2 - 1) as i:
                    sp.wait_ge(w_lo, 4 * i + 4)
                    sp.dma_start(w1_raw[:], w1_v[:, ds(2 * i + 2, 2), :]).then_inc(w_in, 16)
                    sp.dma_start(w2_raw[:], w2_v[:, ds(2 * i + 2, 2), :, :]).then_inc(w_in, 16)
                    for slot in range(2):
                        sp.wait_ge(gate_done, 4 * i + 2 * slot + 2)
                        load_row(2 * i + 2 + slot, slot)

                for b in range(B):
                    sp.wait_ge(f_out, TT * (b + 1))
                    sp.dma_start(out_v[:, b * TT:(b + 1) * TT, :], outs[:, b]).then_inc(stored, 16)
                sp.wait_ge(stored, 16 * B)

            @block.gpsimd
            def _(pool):
                for e in range(E):
                    pool.memset(order[:, e:e + 1], float(E - e)).then_inc(order_set, 1)
                pool.memset(euler[:], math.e).then_inc(order_set, 1)
                pool.wait_ge(order_set, E + 1)
                pool.wait_ge(below_set, 1)
                pool.tensor_tensor(top[:, 5], euler[:], top[:, 4], ALU.pow).then_inc(below_exp, 1)
                for b in range(B):
                    v = xs[:, b * TT:(b + 1) * TT, :]
                    pool.tensor_tensor(v, v, bias_out[:, b:b + 1, :].to_broadcast([P, TT, C]), ALU.add).then_inc(xo_set, 1)

                def add(e, half):
                    pool.wait_ge(gate_done, 2 * e + half + 1)
                    if not (isinstance(e, int) and e == 0):
                        pool.wait_ge(acc_done, 2 * e + half - 1)
                    a = acc[:, half * HALF:(half + 1) * HALF]
                    if isinstance(e, int) and e == 0:
                        pool.tensor_copy(a, gated[:, half, :]).then_inc(acc_done, 1)
                    else:
                        pool.tensor_tensor(a, a, gated[:, half, :], ALU.add).then_inc(acc_done, 1)

                add(0, 0)
                add(0, 1)
                with pool.Fori(1, E - 1) as e:
                    add(e, 0)
                    add(e, 1)
                for b in range(B):
                    pool.wait_ge(f_var, b + 1)
                    pool.tensor_tensor(rstd[:, b], vare[:, b], half_neg[:, 0:TT], ALU.pow).then_inc(f_rstd, 1)
                    if b < B - 1:
                        pool.wait_ge(f_centred, TT * (b + 1))
                        pool.tensor_tensor(outs[:, b], outs[:, b], gate_out[:, b:b + 1, :].to_broadcast([P, TT, C]),
                                           ALU.mult).then_inc(f_gated, 1)

            @block.tensor
            def _(pe):
                def first(i, u):
                    e, half, k = u // UE, u // FC % 2, u % FC
                    if u % UE == 0:
                        pe.wait_ge(w_lo, 4 * i + 2 * e + 1)
                    if isinstance(i, int) and i == 0:
                        if u >= 2:
                            pe.wait_ge(gelu_hi, u - 1)
                    else:
                        pe.wait_ge(gelu_hi, 2 * UE * i + u - 1)
                    for tb in range(2):
                        cols_ = slice(half * HALF + tb * 512, half * HALF + (tb + 1) * 512)
                        for n, (w, h) in enumerate(((w1_hi, h2_hi), (w1_hi, h2_lo), (w1_lo, h2_hi))):
                            mm = pe.matmul(H1[:, u % 2, tb * 512:(tb + 1) * 512], w[:, e, k * P:(k + 1) * P], h[:, cols_],
                                           start=(n == 0), stop=(n == 2))
                    mm.then_inc(h_ps, 1)

                def second(i, u):
                    e, half, k = u // UE, u // FC % 2, u % FC
                    pe.wait_ge(lo_set, 2 * UE * i + u + 1)
                    if u % UE == 0:
                        pe.wait_ge(w_lo, 4 * i + 2 * e + 2)
                    if k == 0:
                        done = 2 * e + half - 1
                        if not (isinstance(i, int) and 4 * i + done <= 0):
                            pe.wait_ge(gate_done, 4 * i + done)
                    for tb in range(2):
                        for n, (w, h) in enumerate(((w2_hi, act_hi), (w2_hi, act_lo), (w2_lo, act_hi))):
                            mm = pe.matmul(Y[:, half, tb * 512:(tb + 1) * 512], w[:, e, k, :],
                                           h[:, u % SLOTS, tb * 512:(tb + 1) * 512],
                                           start=(k == 0 and n == 0), stop=(k == FC - 1 and n == 2), skip_group_check=True)
                    mm.then_inc(mm2, 1)

                for u in range(LAG):
                    first(0, u)
                for u in range(2 * UE):
                    if u == FC - 1:
                        pe.wait_ge(gates_set, 1)
                        pe.transpose(Y[:, 1, P:P + E], b2_rows[:], ident[0:E, 0:E])
                        pe.transpose(Y[:, 1, 0:P], gates[:].rearrange("p t e -> p (t e)"), ident[:]).then_inc(gT_ps, 1)
                    if u == FC:
                        pe.wait_ge(gT_set, 2)
                    second(0, u)
                    first(u // (2 * UE) if u + LAG < 2 * UE else 1, (u + LAG) % (2 * UE))
                with pe.Fori(1, E // 2 - 1) as i:
                    for u in range(2 * UE):
                        second(i, u)
                        first(i if u + LAG < 2 * UE else i + 1, (u + LAG) % (2 * UE))
                last = E // 2 - 1

                def turn_out(b):
                    if b % 2 == 0:
                        pe.wait_ge(acc_done, 2 * E - 3 + b // 2)
                    pe.wait_ge(gate_done, 2 * E - 2 + b + 1)
                    for t in range(TT):
                        o = Y[:, b // 2, (b % 2) * 512 + t * P:(b % 2) * 512 + (t + 1) * P]
                        at = (b * TT + t) * P
                        pe.matmul(o, acc[:, at:at + P], ident[:], start=True, stop=False)
                        mm = pe.matmul(o, gated[:, b // 2, at - (b // 2) * HALF:at - (b // 2) * HALF + P], ident[:], start=False, stop=True)
                    mm.then_inc(outT_ps, 1)

                for u in range(2 * UE):
                    second(last, u)
                    if u + LAG < 2 * UE:
                        first(last, u + LAG)
                    if u == 2 * UE - 2:
                        turn_out(0)
                turn_out(1)
                turn_out(2)
                turn_out(3)

            @block.scalar
            def _(act):
                def gelu(i, u):
                    e, half, k = u // UE, u // FC % 2, u % FC
                    n = 2 * UE * i + u
                    bias = cols[:, ds(2 * FC * i + FC * e + k)]
                    wait_apart(act, h_ps, n + 1)
                    if not (isinstance(i, int) and n < 2):
                        wait_apart(act, lo_set, n - 1)
                    act.activation(act_full[:, u % 2, :], H1[:, u % 2, :], ACT.Gelu, bias=bias).then_inc(gelu_full, 1)
                    if not (isinstance(i, int) and n < SLOTS):
                        wait_apart(act, mm2, n - SLOTS + 1)
                    act.activation(act_hi[:, u % SLOTS, :], H1[:, u % 2, :], ACT.Gelu, bias=bias).then_inc(gelu_hi, 1)

                for u in range(2 * UE):
                    gelu(0, u)
                with act.Fori(1, E // 2) as i:
                    for u in range(2 * UE):
                        gelu(i, u)
                for b in range(B - 1):
                    act.wait_ge(f_mean, b + 1)
                    for t in range(TT):
                        act.activation(outs[:, b, t, :], Y[:, b // 2, (b % 2) * 512 + t * C:(b % 2) * 512 + (t + 1) * C],
                                       ACT.Identity, bias=neg_mean[:, b, t:t + 1]).then_inc(f_centred, 1)

            @block.vector
            def _(dve):
                def split(i, e):
                    if e == 0:
                        dve.wait_ge(w_in, 32 * (i + 1))
                    if not (isinstance(i, int) and i == 0):
                        dve.wait_ge(mm2, 2 * UE * (i - 1) + UE * (e + 1))
                    if not (isinstance(i, int) and i == 0 and e == 0):
                        dve.tensor_copy(w1_hi[:, e, :], w1_raw[:, e, :]).then_inc(w_hi, 1)
                        dve.wait_ge(w_hi, 4 * i + 2 * e + 1)
                        dve.tensor_tensor(w1_lo[:, e, :], w1_raw[:, e, :], w1_hi[:, e, :].bitcast(F32), ALU.subtract).then_inc(w_lo, 1)
                    dve.tensor_copy(w2_hi[:, e], w2_raw[:, e]).then_inc(w_hi, 1)
                    dve.wait_ge(w_hi, 4 * i + 2 * e + 2)
                    dve.tensor_tensor(w2_lo[:, e], w2_raw[:, e], w2_hi[:, e].bitcast(F32), ALU.subtract).then_inc(w_lo, 1)

                count = 0

                def then(ins):
                    nonlocal count
                    count += 1
                    ins.then_inc(step, 1)
                    dve.wait_ge(step, count)

                def wide(v):
                    return v.unsqueeze(2).to_broadcast([P, NT, E])

                lg, sel1, rest, sel2, tmp, gate1 = (pick[:, n] for n in range(6))
                first_, second_ = top[:, 0], top[:, 2]
                below, weight, total, share1, share2 = (top[:, n] for n in range(4, 9))

                def chosen(src, n, sel):
                    then(dve.tensor_tensor(tmp, src, wide(top[:, n]), ALU.is_ge))
                    then(dve.tensor_tensor(tmp, tmp, order[:].unsqueeze(1).to_broadcast([P, NT, E]), ALU.mult))
                    then(dve.tensor_reduce(top[:, n + 1], tmp, AX.X, ALU.max))
                    then(dve.tensor_tensor(sel, tmp, wide(top[:, n + 1]), ALU.is_ge))

                def gates_first():
                    then(dve.tensor_scalar(lg, logits[:], 1.0 / TEMP, None, ALU.mult))
                    then(dve.tensor_reduce(first_, lg, AX.X, ALU.max))
                    dve.wait_ge(order_set, E)
                    chosen(lg, 0, sel1)
                    then(dve.scalar_tensor_tensor(out=rest, in0=sel1, scalar=LOWEST, in1=lg, op0=ALU.mult, op1=ALU.add))
                    then(dve.tensor_reduce(second_, rest, AX.X, ALU.max))
                    dve.tensor_tensor(below, second_, first_, ALU.subtract).then_inc(below_set, 1)

                def gates_second():
                    chosen(rest, 2, sel2)

                def gates_shares():
                    dve.wait_ge(below_exp, 1)
                    then(dve.tensor_scalar(total, weight, 1.0, None, ALU.add))
                    then(dve.reciprocal(share1, total))
                    dve.tensor_tensor(gate1, sel1, wide(share1), ALU.mult)
                    then(dve.tensor_tensor(share2, weight, share1, ALU.mult))
                    then(dve.tensor_tensor(tmp, sel2, wide(share2), ALU.mult))
                    dve.tensor_tensor(gates[:], gate1, tmp, ALU.add).then_inc(gates_set, 1)

                def gates_out():
                    dve.wait_ge(gT_ps, 1)
                    dve.tensor_copy(gates_turned[:], Y[:, 1, 0:P]).then_inc(gT_set, 1)
                    dve.tensor_copy(b2_cols[:], Y[:, 1, P:P + E]).then_inc(gT_set, 1)
                    dve.wait_ge(gT_set, 2)

                def low(i, u):
                    n = 2 * UE * i + u
                    dve.wait_ge(gelu_hi, n + 1)
                    dve.wait_ge(gelu_full, n + 1)
                    if not (isinstance(i, int) and n < SLOTS):
                        dve.wait_ge(mm2, n - SLOTS + 1)
                    dve.tensor_tensor(act_lo[:, u % SLOTS, :], act_full[:, u % 2, :], act_hi[:, u % SLOTS, :].bitcast(F32),
                                      ALU.subtract).then_inc(lo_set, 1)

                def gate(i, g):
                    e, half = g // 2, g % 2
                    wait_apart(dve, mm2, 2 * UE * i + FC * (g + 1))
                    if half == 0:
                        wait_apart(dve, row_in[e], 16 * (i + 1))
                    if not (isinstance(i, int) and i == 0 and e == 0):
                        wait_apart(dve, acc_done, 4 * i + g - 1)
                    dve.scalar_tensor_tensor(out=gated[:, half, :], in0=Y[:, half, :], scalar=b2_cols[:, ds(2 * i + e)],
                                             in1=gate_row[:, e, half * HALF:(half + 1) * HALF], op0=ALU.add,
                                             op1=ALU.mult).then_inc(gate_done, 1)

                def pair(i, first_pair=False, last_pair=False):
                    for u in range(2 * UE):
                        if u == (5 if first_pair else 2):
                            split(i, 1)
                        if u == 11 and not last_pair:
                            split(i + 1, 0)
                        if first_pair and u < 3:
                            (gates_first, gates_second, gates_shares)[u]()
                        if first_pair and u == FC:
                            gates_out()
                        if last_pair and u == 2 * UE - 1:
                            gate_batch(0)
                        low(i, u)
                        if u > FC and (u - LAG) % FC == 0:
                            if last_pair and u > LAG + 2 * FC:
                                gate_batch(1)
                            else:
                                gate(i, (u - LAG) // FC - 1)
                        if u == LAG and not first_pair:
                            gate(i - 1, 3)

                def gate_batch(b):
                    dve.wait_ge(mm2, 2 * UE * (E // 2) - (FC if b < 2 else 0))
                    if b == 0:
                        dve.wait_ge(row_in[1], 16 * (E // 2))
                    if b % 2 == 0:
                        dve.wait_ge(acc_done, 2 * E - 3 + b // 2)
                    half, at = b // 2, (b % 2) * 512
                    dve.scalar_tensor_tensor(out=gated[:, half, at:at + 512], in0=Y[:, half, at:at + 512],
                                             scalar=b2_cols[:, E - 1:E], in1=gate_row[:, 1, b * 512:(b + 1) * 512],
                                             op0=ALU.add, op1=ALU.mult).then_inc(gate_done, 1)

                split(0, 0)
                pair(0, first_pair=True)
                with dve.Fori(1, E // 2 - 1) as i:
                    pair(i)
                pair(E // 2 - 1, last_pair=True)

                def y_of(b):
                    return Y[:, b // 2, (b % 2) * 512:(b % 2 + 1) * 512].rearrange("p (t c) -> p t c", c=C)

                def out_stats(b):
                    dve.wait_ge(outT_ps, b + 1)
                    for t in range(TT):
                        dve.bn_stats(stats[:, t, :], y_of(b)[:, t, :]).then_inc(f_stat, 1)
                    for t in range(TT):
                        dve.wait_ge(f_stat, TT * b + t + 1)
                        dve.bn_aggr(mv[:, b, t, :], stats[:, t, :]).then_inc(f_aggr, 1)
                    dve.wait_ge(f_aggr, TT * b + TT)
                    dve.tensor_scalar(vare[:, b], mv[:, b, :, 1], EPS, None, ALU.add).then_inc(f_var, 1)
                    dve.tensor_scalar(neg_mean[:, b], mv[:, b, :, 0], -1.0, None, ALU.mult).then_inc(f_mean, 1)

                def out_gate(b):
                    for t in range(TT):
                        dve.scalar_tensor_tensor(out=outs[:, b, t, :], in0=y_of(b)[:, t, :], scalar=mv[:, b, t, 0:1],
                                                 in1=gate_out[:, b, :], op0=ALU.subtract, op1=ALU.mult).then_inc(f_gated_last, 1)

                def out_final(b):
                    dve.wait_ge(f_rstd, b + 1)
                    dve.wait_ge(xo_set, b + 1)
                    for t in range(TT):
                        if b == B - 1:
                            dve.wait_ge(f_gated_last, t + 1)
                        else:
                            dve.wait_ge(f_gated, b + 1)
                        dve.scalar_tensor_tensor(out=outs[:, b, t, :], in0=outs[:, b, t, :], scalar=rstd[:, b, t:t + 1],
                                                 in1=xs[:, b * TT + t, :], op0=ALU.mult, op1=ALU.add).then_inc(f_out, 1)

                out_stats(0)
                gate_batch(2)
                gate_batch(3)
                out_stats(1)
                out_stats(2)
                out_final(0)
                out_stats(3)
                out_final(1)
                out_gate(3)
                out_final(2)
                out_final(3)


_INS = ["L0_attn_x", "L0_attn_Wq", "L0_attn_bq", "L0_attn_Wk", "L0_attn_bk", "L0_attn_Wv", "L0_attn_bv",
        "L0_attn_Wo", "L0_attn_bo", "L0_attn_gamma", "L0_attn_beta", "L0_ffn_gate_w", "L0_ffn_gate_b",
        "L0_ffn_w1", "L0_ffn_b1", "L0_ffn_w2", "L0_ffn_b2", "L0_ffn_ln_g", "L0_ffn_ln_b", "L0_c", "L0_wmod"]


def kernel(**inputs):
    import numpy as np
    import concourse.bacc as bacc
    from concourse.bass_utils import run_bass_kernel_spmd

    nc = bacc.Bacc("TRN2", target_bir_lowering=False, num_devices=1)
    arrays, args = {}, []
    for name in _INS:
        a = np.ascontiguousarray(inputs[name])
        arrays[f"in_{name}"] = a
        args.append(nc.dram_tensor(f"in_{name}", a.shape, mybir.dt.from_np(a.dtype), kind="ExternalInput").ap())
    shape = inputs["L0_attn_x"].shape
    args.append(nc.dram_tensor("out_x", shape, F32, kind="ExternalOutput").ap())
    build(nc, *args)
    r = run_bass_kernel_spmd(nc, [arrays], core_ids=[0])
    return r.results[0]["out_x"]
```
